# Optimizing a Trainium2 kernel written in Bass

```python
import numpy as np
import jax
import jax.numpy as jnp

def _softmax(x, axis=-1):
    return jax.nn.softmax(x, axis=axis)

def _gelu(x):
    return jax.nn.gelu(x, approximate=True)

def _silu(x):
    return jax.nn.silu(x)

def _sigmoid(x):
    return jax.nn.sigmoid(x)

def _layernorm(x, axis=-1, eps=1e-05):
    m = jnp.mean(x, axis=axis, keepdims=True)
    v = jnp.var(x, axis=axis, keepdims=True)
    return (x - m) / jnp.sqrt(v + eps)

def _scatter_add(tgt, idx, src, axis=0):
    return tgt.at[idx].add(src)

def _segment_sum(src, seg, n):
    return jax.ops.segment_sum(src, seg, n)
kernel_name = 'mk_seq_preln_d1_jaxref_r4_f8d974'

def setup_inputs(seed: int=0):
    np.random.seed(seed)
    _w = jnp.asarray

    def _L0_attn_setup():
        import jax, jax.numpy as jnp
        import numpy as np
        D_MODEL = 256
        N_HEADS = 16
        HEAD_DIM = 64
        RANK = 8
        RIDGE_EPS = 0.0001
        SCALE = 0.125
        POWER_K = 2
        CHUNK = 128
        DECAY_ALPHA = 0.9
        LN_EPS = 1e-05

        def _layernorm(x, g, b):
            mu = jnp.mean(x, axis=-1, keepdims=True)
            var = jnp.mean(jnp.square(x - mu), axis=-1, keepdims=True)
            return (x - mu) * jax.lax.rsqrt(var + LN_EPS) * g + b

        def _ska_per_lane(q, k, v):
            Dh = q.shape[-1]
            I = jnp.eye(Dh, dtype=q.dtype)
            U0 = I[:, :RANK]

            def step(S, qkv):
                Qc, Kc, Vc = qkv
                G = Kc.T @ Kc + RIDGE_EPS * I
                W = jnp.linalg.solve(G, Kc.T @ Vc)
                U = U0
                for _ in range(POWER_K):
                    U, _ = jnp.linalg.qr(W @ U)
                Wr = U @ (U.T @ W)
                S_new = DECAY_ALPHA * S + Wr
                out = SCALE * (Qc @ S_new)
                return (S_new, out)
            S0 = jnp.zeros((Dh, Dh), dtype=q.dtype)
            _, outs = jax.lax.scan(step, S0, (q, k, v))
            return outs

        def _ska_block(x, ln_g, ln_b, Wq, Wk, Wv, Wo):
            B, S, _ = x.shape
            N = S // CHUNK
            xn = _layernorm(x, ln_g, ln_b)

            def to_lanes(W):
                h = xn @ W
                h = h.reshape(B, S, N_HEADS, HEAD_DIM)
                h = jnp.transpose(h, (0, 2, 1, 3))
                return h.reshape(B * N_HEADS, N, CHUNK, HEAD_DIM)
            q, k, v = (to_lanes(Wq), to_lanes(Wk), to_lanes(Wv))
            o = jax.vmap(_ska_per_lane)(q, k, v)
            o = o.reshape(B, N_HEADS, S, HEAD_DIM)
            o = jnp.transpose(o, (0, 2, 1, 3)).reshape(B, S, N_HEADS * HEAD_DIM)
            return x + o @ Wo
        key = jax.random.key(seed)
        ks = jax.random.split(key, 5)
        B, S = (2, 1024)
        x = jax.random.normal(ks[0], (B, S, D_MODEL), dtype=jnp.float32)
        w_std = 0.02
        Wq = jax.random.normal(ks[1], (D_MODEL, N_HEADS * HEAD_DIM), dtype=jnp.float32) * w_std
        Wk = jax.random.normal(ks[2], (D_MODEL, N_HEADS * HEAD_DIM), dtype=jnp.float32) * w_std
        Wv = jax.random.normal(ks[3], (D_MODEL, N_HEADS * HEAD_DIM), dtype=jnp.float32) * w_std
        Wo = jax.random.normal(ks[4], (N_HEADS * HEAD_DIM, D_MODEL), dtype=jnp.float32) * w_std
        ln_g = jnp.ones((D_MODEL,), dtype=jnp.float32)
        ln_b = jnp.zeros((D_MODEL,), dtype=jnp.float32)
        return {'x': x, 'ln_g': ln_g, 'ln_b': ln_b, 'Wq': Wq, 'Wk': Wk, 'Wv': Wv, 'Wo': Wo}
    _L0_attn_in = _L0_attn_setup()

    def _L0_ffn_setup():
        import jax, jax.numpy as jnp
        import numpy as np

        def _binarize(w):
            alpha = jax.lax.stop_gradient(jnp.mean(jnp.abs(w), axis=1, keepdims=True))
            bw = alpha * jnp.sign(w)
            return w + jax.lax.stop_gradient(bw - w)
        key = jax.random.key(seed)
        k1, k2, k3, k4, k5 = jax.random.split(key, 5)
        D, H = (256, 1024)
        x = jax.random.normal(k1, (64, 196, D), dtype=jnp.float32)
        w1 = jax.random.normal(k2, (H, D), dtype=jnp.float32) * 0.02
        b1 = jax.random.normal(k3, (H,), dtype=jnp.float32) * 0.02
        w2 = jax.random.normal(k4, (D, H), dtype=jnp.float32) * 0.02
        b2 = jax.random.normal(k5, (D,), dtype=jnp.float32) * 0.02
        return {'x': x, 'w1': w1, 'b1': b1, 'w2': w2, 'b2': b2}
    _L0_ffn_in = _L0_ffn_setup()
    _d = {'L0_attn_x': _L0_attn_in['x'], 'L0_attn_ln_g': _L0_attn_in['ln_g'], 'L0_attn_ln_b': _L0_attn_in['ln_b'], 'L0_attn_Wq': _L0_attn_in['Wq'], 'L0_attn_Wk': _L0_attn_in['Wk'], 'L0_attn_Wv': _L0_attn_in['Wv'], 'L0_attn_Wo': _L0_attn_in['Wo'], 'L0_ffn_w1': _L0_ffn_in['w1'], 'L0_ffn_b1': _L0_ffn_in['b1'], 'L0_ffn_w2': _L0_ffn_in['w2'], 'L0_ffn_b2': _L0_ffn_in['b2']}
    _x0 = _d['L0_attn_x']
    _d['L0_attn_x'] = jax.random.normal(jax.random.fold_in(jax.random.key(seed), 1), (4, 1024, 256), dtype=_x0.dtype)
    del _x0
    return _d

def reference(L0_attn_x, L0_attn_ln_g, L0_attn_ln_b, L0_attn_Wq, L0_attn_Wk, L0_attn_Wv, L0_attn_Wo, L0_ffn_w1, L0_ffn_b1, L0_ffn_w2, L0_ffn_b2):

    def _L0_attn_ref(x, ln_g, ln_b, Wq, Wk, Wv, Wo):
        import jax, jax.numpy as jnp
        import numpy as np
        D_MODEL = 256
        N_HEADS = 16
        HEAD_DIM = 64
        RANK = 8
        RIDGE_EPS = 0.0001
        SCALE = 0.125
        POWER_K = 2
        CHUNK = 128
        DECAY_ALPHA = 0.9
        LN_EPS = 1e-05

        def _layernorm(x, g, b):
            mu = jnp.mean(x, axis=-1, keepdims=True)
            var = jnp.mean(jnp.square(x - mu), axis=-1, keepdims=True)
            return (x - mu) * jax.lax.rsqrt(var + LN_EPS) * g + b

        def _ska_per_lane(q, k, v):
            Dh = q.shape[-1]
            I = jnp.eye(Dh, dtype=q.dtype)
            U0 = I[:, :RANK]

            def step(S, qkv):
                Qc, Kc, Vc = qkv
                G = Kc.T @ Kc + RIDGE_EPS * I
                W = jnp.linalg.solve(G, Kc.T @ Vc)
                U = U0
                for _ in range(POWER_K):
                    U, _ = jnp.linalg.qr(W @ U)
                Wr = U @ (U.T @ W)
                S_new = DECAY_ALPHA * S + Wr
                out = SCALE * (Qc @ S_new)
                return (S_new, out)
            S0 = jnp.zeros((Dh, Dh), dtype=q.dtype)
            _, outs = jax.lax.scan(step, S0, (q, k, v))
            return outs

        def _ska_block(x, ln_g, ln_b, Wq, Wk, Wv, Wo):
            B, S, _ = x.shape
            N = S // CHUNK
            xn = _layernorm(x, ln_g, ln_b)

            def to_lanes(W):
                h = xn @ W
                h = h.reshape(B, S, N_HEADS, HEAD_DIM)
                h = jnp.transpose(h, (0, 2, 1, 3))
                return h.reshape(B * N_HEADS, N, CHUNK, HEAD_DIM)
            q, k, v = (to_lanes(Wq), to_lanes(Wk), to_lanes(Wv))
            o = jax.vmap(_ska_per_lane)(q, k, v)
            o = o.reshape(B, N_HEADS, S, HEAD_DIM)
            o = jnp.transpose(o, (0, 2, 1, 3)).reshape(B, S, N_HEADS * HEAD_DIM)
            return x + o @ Wo
        return _ska_block(x, ln_g, ln_b, Wq, Wk, Wv, Wo)

    def _L0_ffn_ref(x, w1, b1, w2, b2):
        import jax, jax.numpy as jnp
        import numpy as np

        def _binarize(w):
            alpha = jax.lax.stop_gradient(jnp.mean(jnp.abs(w), axis=1, keepdims=True))
            bw = alpha * jnp.sign(w)
            return w + jax.lax.stop_gradient(bw - w)
        bw1 = _binarize(w1)
        h = jnp.einsum('bsd,hd->bsh', x, bw1) + b1
        h = jax.nn.gelu(h, approximate=False)
        bw2 = _binarize(w2)
        out = jnp.einsum('bsh,dh->bsd', h, bw2) + b2
        return out
    x = L0_attn_x
    x = x + _L0_attn_ref(_layernorm(x, axis=-1), L0_attn_ln_g, L0_attn_ln_b, L0_attn_Wq, L0_attn_Wk, L0_attn_Wv, L0_attn_Wo)
    x = x + _L0_ffn_ref(_layernorm(x, axis=-1), L0_ffn_w1, L0_ffn_b1, L0_ffn_w2, L0_ffn_b2)
    return x

_drawn_inputs = setup_inputs


def setup_inputs(seed=0):
    import zlib

    import numpy as np

    out = dict(_drawn_inputs(seed))
    spreads = {'L0_attn_ln_g': (1.0, 0.6), 'L0_attn_ln_b': (0.0, 0.8)}
    factors = {'L0_attn_Wq': 3.131,
     'L0_attn_Wk': 3.151,
     'L0_attn_Wv': 3.149,
     'L0_attn_Wo': 3.145,
     'L0_ffn_b1': 21.832,
     'L0_ffn_b2': 5.819}
    for name, (base, spread) in spreads.items():
        noise = np.random.default_rng([zlib.crc32(name.encode()), seed]).standard_normal(out[name].shape)
        drawn = base * np.exp(spread * noise) if base else spread * noise
        out[name] = jnp.asarray(drawn.astype(out[name].dtype))
    for name, factor in factors.items():
        out[name] = (out[name] * factor).astype(out[name].dtype)
    return out
```

```python
from contextlib import ExitStack

import concourse.bass as bass
from concourse import mybir

P = 128
ALU = mybir.AluOpType
ACT = mybir.ActivationFunctionType
F32 = mybir.dt.float32

BATCH, SEQ, DM = 4, 1024, 256
HEADS, HD, RANK = 16, 64, 8
CHUNK = P
CPB = SEQ // CHUNK
NCH = BATCH * CPB
PAIRS = HEADS // 2
KT = DM // P
HALF = HD // 2
FF = 1024
FT = FF // P
BANK = 512

RIDGE, LN_EPS, SCALE, DECAY = 1e-4, 1e-5, 0.125, 0.9
GROUP = 4

SWEEPS = [(0, 0), (0, 1), (1, 0), (0, 2), (1, 1), (0, 3), (1, 2), (1, 3)]
FIRST_PHASE = [("project", 0), ("project", 1), ("schur", 0), ("project", 2), ("schur", 1),
               ("project", 3), ("schur", 2), ("schur", 3)]


def build(nc, x, ln_g, ln_b, Wq, Wk, Wv, Wo, w1, b1, w2, b2, out):
    x_rows = x.rearrange("b s d -> (b s) d")
    x_groups = x_rows.rearrange("(g k p) d -> g p k d", p=P, k=GROUP)
    out_chunks = out.rearrange("b s d -> (b s) d").rearrange("(c p) d -> c p d", p=P)

    def scratch(name, shape):
        return nc.dram_tensor(name, shape, F32, kind="Internal").ap()

    xhat_d = scratch("xhat_d", [NCH, P, DM])
    res_d = scratch("res_d", [NCH, P, DM])
    gc_d = scratch("gc_d", [2 * NCH, HD, PAIRS, 2 * HD])
    q_d = scratch("q_d", [NCH, P, PAIRS, P])
    schur_d = scratch("schur_d", [2 * NCH, HD, PAIRS, HALF])
    inv_d = [scratch(f"inv{k}_d", [2 * NCH, PAIRS, HALF, HALF]) for k in range(2)]
    z_d = scratch("z_d", [NCH, 2 * RANK, PAIRS * HD])
    yt_d = scratch("yt_d", [NCH, 2 * RANK, PAIRS * P])
    m_d = scratch("m_d", [NCH, 2, RANK, PAIRS, 2 * RANK])
    minv_d = scratch("minv_d", [2 * NCH, PAIRS, RANK, RANK])

    with ExitStack() as ctx:
        def sb(name, shape, dt=F32):
            return ctx.enter_context(nc.sbuf_tensor(name, shape, dt))

        def sem(name):
            return ctx.enter_context(nc.semaphore(name))

        bank = [ctx.enter_context(nc.psum_tensor(f"bank{n}", [P, BANK], F32)) for n in range(8)]

        wqkv = sb("wqkv", [P, 3, KT, HEADS * HD])
        wo = sb("wo", [P, PAIRS, DM])
        s1t = sb("s1t", [P, KT, FF])
        s2t = sb("s2t", [P, FT, DM])
        ident = sb("ident", [P, P])
        ones = sb("ones", [P, P])
        diag = sb("diag", [P, KT, P])
        gain = sb("gain", [P, KT])
        bias = sb("bias", [P, KT])
        b1c = sb("b1c", [P, FT])
        b2r = sb("b2r", [P, DM])
        alpha1 = sb("alpha1", [P, FT])
        alpha2 = sb("alpha2", [P, KT])
        alpha2r = sb("alpha2r", [P, DM])
        half_neg = sb("half_neg", [P, GROUP])
        work = sb("work", [P, 4, HALF * HALF])
        w1n = work[:, 0:2, :].rearrange("p a n -> p (a n)").rearrange("p (t d) -> p t d", d=DM)
        w2n = work[:, 2:4, :]
        early = sb("early", [P, 3 * 2 * GROUP * DM])
        xg, lng, hatg = (early[:, 2 * GROUP * DM * n:2 * GROUP * DM * (n + 1)].rearrange(
            "p (a k d) -> p a k d", a=2, k=GROUP) for n in range(3))
        stats = sb("stats", [P, GROUP, 6])
        mv = sb("mv", [P, GROUP, 2])
        mv2 = sb("mv2", [P, GROUP, 2])
        veps = sb("veps", [P, GROUP])
        veps2 = sb("veps2", [P, GROUP])
        rstd = sb("rstd", [P, GROUP])
        rstd2 = sb("rstd2", [P, GROUP])
        xh = sb("xh", [P, 2, DM])
        xnt = sb("xnt", [P, 2, KT, P])
        kv = sb("kv", [P, 2, 2, HEADS * HD])
        absw = kv[:, 0, 0, :]
        qt = sb("qt", [P, 2, PAIRS, P])
        gc = sb("gc", [P, 2, PAIRS, 2 * HD])
        gct = sb("gct", [P, 2, PAIRS, 2 * HD])
        gbd = sb("gbd", [P, 2, PAIRS, P])
        pbd = sb("pbd", [P, 2, PAIRS, P])
        sbd = sb("sbd", [P, 2, PAIRS, P])
        xs = sb("xs", [P, PAIRS, HALF])
        sch = sb("sch", [P, 2, PAIRS, HALF])
        upper = sb("upper", [P, HALF, HALF])
        lower = sb("lower", [P, HALF, HALF])
        piv = sb("piv", [P, 1])
        prow = sb("prow", [P, HALF])
        outer = sb("outer", [P, 16 * 31 + 15 * 15])
        used = [0]

        def late(*dims):
            size = 1
            for n in dims:
                size *= n
            part = early[:, used[0]:used[0] + size]
            used[0] += size
            assert used[0] <= early.shape[1]
            return part.rearrange("p (a b) -> p a b", a=dims[0]) if len(dims) == 2 else part

        ysb, rsb, w2sb, r2sb, wt = (late(PAIRS, HD) for _ in range(5))
        wbd = sb("wbd", [P, PAIRS, P])
        wbdt = late(PAIRS, P)
        y2bd = sb("y2bd", [P, PAIRS, 2 * RANK])
        zs = kv[0:2 * RANK, 1, 0, :].rearrange("p (a n) -> p a n", a=2)
        yts = gc[0:2 * RANK].rearrange("p a h n -> p a (h n)")
        ms = sb("ms", [2 * RANK, 2, PAIRS * 2 * RANK])
        msw = sb("msw", [P, 2, RANK, RANK])
        zl = sb("zl", [2 * RANK, 2, PAIRS, HD])
        ytl = sb("ytl", [2 * RANK, 2, PAIRS, P])
        mbd = sb("mbd", [2 * RANK, 2, PAIRS, 2 * RANK])
        nz = sb("nz", [2 * RANK, PAIRS, HD])
        state = sb("state", [P, 2, PAIRS, P])
        ot = kv[:, 0, 0, :].rearrange("p (h r) -> p h r", h=PAIRS)
        ht = kv[:, 0, 1, :].rearrange("p (t r) -> p t r", t=FT)
        resl = late(2, DM)
        x2, x2b, x3, ysc = (late(DM) for _ in range(4))
        st3 = sb("st3", [P, 6])
        mv3 = sb("mv3", [P, 2])
        ve3 = sb("ve3", [P, 1])
        rs3 = sb("rs3", [P, 1])
        y3t = late(KT, P)
        yo = late(2, DM)

        consts_loaded = sem("consts_loaded")
        qkv_loaded = sem("qkv_loaded")
        ffw_loaded = sem("ffw_loaded")
        b2_loaded = sem("b2_loaded")
        zeroed = sem("zeroed")
        abs_done = sem("abs_done")
        alpha_done = sem("alpha_done")
        sign_done = sem("sign_done")
        diag_done = sem("diag_done")
        sgn_ready = sem("sgn_ready")
        sgn_copied = sem("sgn_copied")
        alpha_bcast = sem("alpha_bcast")
        alpha_row = sem("alpha_row")
        x_loaded = [sem(f"x_loaded{n}") for n in range(2)]
        ln_step = sem("ln_step")
        veps_ready = sem("veps_ready")
        rstd_ready = sem("rstd_ready")
        hat_ready = sem("hat_ready")
        ln_stored = [sem(f"ln_stored{n}") for n in range(BATCH)]
        xhat_loaded = [sem(f"xhat_loaded{n}") for n in range(2)]
        xnt_ready = sem("xnt_ready")
        xnt_copied = sem("xnt_copied")
        kvq_ready = sem("kvq_ready")
        kvq_copied = sem("kvq_copied")
        gc_ready = sem("gc_ready")
        gc_copied = sem("gc_copied")
        gc_stored = [sem(f"gc_stored{n}") for n in range(2)]
        q_stored = [sem(f"q_stored{n}") for n in range(2)]
        blocks_loaded = [sem(f"blocks_loaded{n}") for n in range(2)]
        t_ready = sem("t_ready")
        t_copied = sem("t_copied")
        schur_ready = sem("schur_ready")
        schur_copied = sem("schur_copied")
        schur_stored = [sem(f"schur_stored{n}") for n in range(2)]
        sweep_loaded = [sem(f"sweep_loaded{n}") for n in range(2)]
        swept = sem("swept")
        inverted = sem("inverted")
        mirrored = sem("mirrored")
        inv_stored = [sem(f"inv_stored{k}") for k in range(len(SWEEPS))]
        solve_loaded = [sem(f"solve_loaded{n}") for n in range(2)]
        y_ready, y_copied = sem("y_ready"), sem("y_copied")
        g1_ready, r1_done = sem("g1_ready"), sem("r1_done")
        w2_ready, w2_copied = sem("w2_ready"), sem("w2_copied")
        g2_ready, r2_done = sem("g2_ready"), sem("r2_done")
        w_ready, w_copied = sem("w_ready"), sem("w_copied")
        wbd_copied = sem("wbd_copied")
        wbdt_ready, wbdt_copied = sem("wbdt_ready"), sem("wbdt_copied")
        y2_ready, y2_copied = sem("y2_ready"), sem("y2_copied")
        z_ready, z_copied = sem("z_ready"), sem("z_copied")
        m_ready, m_copied = sem("m_ready"), sem("m_copied")
        yt_ready, yt_copied = sem("yt_ready"), sem("yt_copied")
        factors_stored = [sem(f"factors_stored{n}") for n in range(2)]
        m_loaded = sem("m_loaded")
        m_inverted = sem("m_inverted")
        minv_stored = [sem(f"minv_stored{n}") for n in range(BATCH)]
        apply_loaded = [sem(f"apply_loaded{n}") for n in range(2)]
        nz_ready, nz_copied = sem("nz_ready"), sem("nz_copied")
        wr_ready = sem("wr_ready")
        state_cleared = sem("state_cleared")
        state_done = sem("state_done")
        ot_ready, ot_copied = sem("ot_ready"), sem("ot_copied")
        wo_ready = sem("wo_ready")
        x2_done = sem("x2_done")
        x2b_done = sem("x2b_done")
        ln3_step = sem("ln3_step")
        ve3_ready, rs3_ready, x3_ready = sem("ve3_ready"), sem("rs3_ready"), sem("x3_ready")
        y3t_ready, y3t_copied = sem("y3t_ready"), sem("y3t_copied")
        h_ready, h_copied = sem("h_ready"), sem("h_copied")
        o_ready, scaled, o_done = sem("o_ready"), sem("scaled"), sem("o_done")
        out_stored = [sem(f"out_stored{n}") for n in range(2)]

        block = ctx.enter_context(nc.Block())

        PAIRS_B = CPB // 2

        def wait(eng, s, value):
            if isinstance(value, int) and value <= 0:
                return
            eng.wait_ge(s, value)

        def each_pair(eng, first, last, body):
            if first == 0:
                for par in range(2):
                    body(0, par)
                first = 1
            with eng.Fori(first, last) as i:
                for par in range(2):
                    body(i, par)

        @block.sync
        def _(sp):
            sp.dma_start(gain[:], ln_g.rearrange("(t p) -> p t", p=P), allow_slow_non_contiguous=True).then_inc(consts_loaded, 16)
            sp.dma_start(bias[:], ln_b.rearrange("(t p) -> p t", p=P), allow_slow_non_contiguous=True).then_inc(consts_loaded, 16)
            sp.dma_start(b1c[:], b1.rearrange("(t p) -> p t", p=P), allow_slow_non_contiguous=True).then_inc(consts_loaded, 16)
            sp.dma_start(w1n, w1.rearrange("(t p) d -> p t d", p=P)).then_inc(ffw_loaded, 16)
            sp.dma_start(w2n, w2.rearrange("(t p) h -> p t h", p=P)).then_inc(ffw_loaded, 16)
            for n, w in enumerate((Wk, Wv, Wq)):
                sp.dma_start(wqkv[:, n], w.rearrange("(t p) h -> p t h", p=P)).then_inc(qkv_loaded, 16)
            sp.dma_start(wo[:], Wo.rearrange("(h p) d -> p h d", p=P)).then_inc(qkv_loaded, 16)
            sp.dma_start(b2r[:], b2.rearrange("(a d) -> a d", a=1).broadcast_to([P, DM])).then_inc(b2_loaded, 16)

            def store_gc(i, par):
                wait(sp, gc_copied, 2 * (2 * i + par + 1))
                sp.dma_start(gc_d[bass.ds(2 * (2 * i + par), 2)].rearrange("a r h n -> (a r) h n"),
                             gc[:, par]).then_inc(gc_stored[par], 16)

            def store_q(i, par):
                wait(sp, kvq_copied, 6 * (2 * i + par + 1))
                sp.dma_start(q_d[bass.ds(2 * i + par, 1)].rearrange("a p h r -> (a p) h r"),
                             qt[:, par]).then_inc(q_stored[par], 16)

            def project(i, par, lead):
                c = 2 * i + par
                wait(sp, xnt_ready, c - 1)
                sp.dma_start(xh[:, par], xhat_d[bass.ds(c, 1)].rearrange("a p d -> (a p) d")).then_inc(xhat_loaded[par], 16)
                if not lead or par == 1:
                    if not lead:
                        store_gc(i - 1, par)
                    store_q(i if par else i - 1, 1 - par)

            def blocks(i, par, which, halves, s):
                dst = (pbd, sbd)[which]
                for a in range(2):
                    lo = HD * a + HALF * which
                    sp.dma_start(dst[lo:lo + HALF, par, :, lo:lo + HALF],
                                 inv_d[which][bass.ds(2 * (2 * i + par) + a, 1)].rearrange("a h i j -> (a i) h j")
                                 ).then_inc(s, 16)

            def load_gram(i, par, s):
                c2 = 2 * (2 * i + par)
                sp.dma_start(gct[:, par], gc_d[bass.ds(c2, 2)].rearrange("a r h n -> (a r) h n")).then_inc(s, 16)
                for a in range(2):
                    sp.dma_start(gbd[HD * a:HD * a + HD, par, :, HD * a:HD * a + HD],
                                 gc_d[bass.ds(c2 + a, 1), :, :, 0:HD].rearrange("a r h n -> (a r) h n")).then_inc(s, 16)

            def store_schur(i, par):
                wait(sp, schur_copied, 2 * i + par + 1)
                sp.dma_start(schur_d[bass.ds(2 * (2 * i + par), 2)].rearrange("a r h n -> (a r) h n"),
                             sch[:, par]).then_inc(schur_stored[par], 16)

            def schur(i, par, lead):
                wait(sp, schur_ready, 2 * i + par - 1)
                load_gram(i, par, blocks_loaded[par])
                blocks(i, par, 0, None, blocks_loaded[par])
                if not lead or par == 1:
                    store_schur(i if par else i - 1, 1 - par)

            sp.wait_ge(zeroed, 1)
            for stage, b in FIRST_PHASE:
                first, last = PAIRS_B * b, PAIRS_B * (b + 1)
                if stage == "project":
                    sp.wait_ge(ln_stored[b], 64)
                    for par in range(2):
                        project(first, par, True)
                    with sp.Fori(first + 1, last) as i:
                        for par in range(2):
                            project(i, par, False)
                    store_gc(last - 1, 0)
                    store_q(last - 1, 1)
                    store_gc(last - 1, 1)
                else:
                    for n in range(2):
                        sp.wait_ge(gc_stored[n], 16 * last)
                    sp.wait_ge(inv_stored[SWEEPS.index((0, b))], 16)
                    for par in range(2):
                        schur(first, par, True)
                    with sp.Fori(first + 1, last) as i:
                        for par in range(2):
                            schur(i, par, False)
                    store_schur(last - 1, 1)

            def solve(i, par):
                c = 2 * i + par
                wait(sp, w_ready, c - 1)
                wait(sp, r2_done, c - 1)
                load_gram(i, par, solve_loaded[par])
                blocks(i, par, 0, None, solve_loaded[par])
                blocks(i, par, 1, None, solve_loaded[par])

            def store_factors(i, par):
                c = 2 * i + par
                wait(sp, z_copied, c + 1)
                sp.dma_start(z_d[bass.ds(c, 1)].rearrange("a r n -> (a r) n"), zs[:, par]).then_inc(factors_stored[par], 16)
                wait(sp, m_copied, c + 1)
                sp.dma_start(m_d[bass.ds(c, 1)].rearrange("c a r h n -> (c a r) (h n)"), ms[:, par]).then_inc(factors_stored[par], 16)
                wait(sp, yt_copied, 2 * (c + 1))
                sp.dma_start(yt_d[bass.ds(c, 1)].rearrange("a r n -> (a r) n"), yts[:, par]).then_inc(factors_stored[par], 16)

            def load_apply(i, par):
                c = 2 * i + par
                wait(sp, ot_ready, 2 * (c - 1))
                wait(sp, x2_done, c - 1)
                s = apply_loaded[par]
                sp.dma_start(zl[:, par], z_d[bass.ds(c, 1)].rearrange("a r (h n) -> (a r) h n", h=PAIRS)).then_inc(s, 16)
                sp.dma_start(ytl[:, par], yt_d[bass.ds(c, 1)].rearrange("a r (h n) -> (a r) h n", h=PAIRS)).then_inc(s, 16)
                for a in range(2):
                    lo = RANK * a
                    sp.dma_start(mbd[lo:lo + RANK, par, :, lo:lo + RANK],
                                 minv_d[bass.ds(2 * c + a, 1)].rearrange("a h i j -> (a i) h j")).then_inc(s, 16)
                sp.dma_start(qt[:, par], q_d[bass.ds(c, 1)].rearrange("a p h r -> (a p) h r")).then_inc(s, 16)
                sp.dma_start(resl[:, par], res_d[bass.ds(c, 1)].rearrange("a p d -> (a p) d")).then_inc(s, 16)

            def store_out(i, par):
                c = 2 * i + par
                wait(sp, o_done, c + 1)
                sp.dma_start(out_chunks[bass.ds(c, 1)].rearrange("a p d -> (a p) d"), yo[:, par]).then_inc(out_stored[par], 16)

            sp.wait_ge(schur_ready, NCH)
            for s in (6, 7):
                sp.wait_ge(inv_stored[s], 16)
            for n in range(2):
                sp.wait_ge(q_stored[n], 16 * NCH // 2)

            def solve_only(i, par):
                solve(i, par)
                store_factors(i, par)

            each_pair(sp, 0, PAIRS_B, solve_only)
            for b in range(BATCH):
                sp.wait_ge(minv_stored[b], 16)

                def both(i, par, more=b + 1 < BATCH):
                    if more:
                        solve(i + PAIRS_B, par)
                    load_apply(i, par)
                    if more:
                        store_factors(i + PAIRS_B, par)
                    store_out(i, par)

                each_pair(sp, PAIRS_B * b, PAIRS_B * (b + 1), both)
            for n in range(2):
                sp.wait_ge(out_stored[n], 16 * NCH // 2)
                sp.wait_ge(factors_stored[n], 48 * NCH // 2)

        @block.gpsimd
        def _(pool):
            nc.gpsimd.memset(ident[:], 0.0).then_inc(zeroed, 1)
            pool.wait_ge(zeroed, 1)
            nc.gpsimd.affine_select(out=ident[:], in_=ident[:], compare_op=ALU.not_equal, fill=1.0, base=0,
                                    pattern=[[-1, P]], channel_multiplier=1).then_inc(zeroed, 1)
            nc.gpsimd.memset(half_neg[:], -0.5).then_inc(zeroed, 1)
            nc.gpsimd.memset(ones[:], 1.0).then_inc(zeroed, 1)
            for g in range(2):
                pool.dma_start(xg[:, g], x_groups[g]).then_inc(x_loaded[g], 16)
            for t in (gbd, pbd, sbd, wbd, y2bd, mbd, state):
                nc.gpsimd.memset(t[:], 0.0).then_inc(zeroed, 1)

            for g in range(NCH // GROUP):
                pool.wait_ge(veps_ready, 2 * g + 1)
                nc.gpsimd.tensor_tensor(rstd[:], veps[:], half_neg[:], ALU.pow).then_inc(rstd_ready, 1)
                pool.wait_ge(veps_ready, 2 * g + 2)
                nc.gpsimd.tensor_tensor(rstd2[:], veps2[:], half_neg[:], ALU.pow).then_inc(rstd_ready, 1)
                pool.wait_ge(hat_ready, g + 1)
                b = g * GROUP // CPB
                chunks = slice(g * GROUP, (g + 1) * GROUP)
                pool.dma_start(xhat_d[chunks].rearrange("k p d -> p k d"), hatg[:, g % 2]).then_inc(ln_stored[b], 16)
                pool.dma_start(res_d[chunks].rearrange("k p d -> p k d"), lng[:, g % 2]).then_inc(ln_stored[b], 16)
                if g + 2 < NCH // GROUP:
                    pool.dma_start(xg[:, g % 2], x_groups[g + 2]).then_inc(x_loaded[g % 2], 16)

            def load(k):
                which, b = SWEEPS[k]
                chunks = slice(2 * CPB * b, 2 * CPB * (b + 1))
                for n in range(2):
                    pool.wait_ge((gc_stored, schur_stored)[which][n], 16 * PAIRS_B * (b + 1))
                if k >= 2:
                    pool.wait_ge(mirrored, 3 * (k - 1))
                if which == 0:
                    src = gc_d[chunks, 0:HALF, :, 0:HALF]
                else:
                    src = schur_d[chunks, HALF:HD, :, :]
                dst = work[:, 2 * (k % 2), :]
                for c in range(2 * CPB):
                    pool.dma_start(dst[PAIRS * c:PAIRS * (c + 1), :].rearrange("h (i j) -> h i j", i=HALF),
                                   src[c].rearrange("i h j -> h i j")).then_inc(sweep_loaded[k % 2], 16)

            def finish(k):
                which, b = SWEEPS[k]
                pool.wait_ge(inverted, k + 1)
                if k >= 1:
                    pool.wait_ge(inv_stored[k - 1], 16)
                src = work[:, 2 * (k % 2), :].rearrange("p (i j) -> p i j", i=HALF)
                nc.gpsimd.affine_select(out=upper[:], in_=src, compare_op=ALU.is_ge, fill=0.0, base=0,
                                        pattern=[[-1, HALF], [1, HALF]], channel_multiplier=0).then_inc(mirrored, 1)
                nc.gpsimd.affine_select(out=lower[:], in_=src.rearrange("p i j -> p j i"), compare_op=ALU.is_gt,
                                        fill=0.0, base=0, pattern=[[1, HALF], [-1, HALF]],
                                        channel_multiplier=0).then_inc(mirrored, 1)
                pool.wait_ge(mirrored, 3 * k + 2)
                nc.gpsimd.tensor_tensor(upper[:], upper[:], lower[:], ALU.add).then_inc(mirrored, 1)
                pool.wait_ge(mirrored, 3 * k + 3)
                pool.dma_start(inv_d[which][2 * CPB * b:2 * CPB * (b + 1)].rearrange("c h i j -> (c h) (i j)"),
                               upper[:].rearrange("p i j -> p (i j)")).then_inc(inv_stored[k], 16)

            pool.wait_ge(sgn_copied, 8)
            load(0)
            finish(0)
            load(1)
            for k in range(2, len(SWEEPS)):
                load(k)
                finish(k - 1)
            finish(len(SWEEPS) - 1)

            def norm3(i, par):
                c = 2 * i + par
                wait(pool, ve3_ready, c + 1)
                nc.gpsimd.tensor_tensor(rs3[:], ve3[:], half_neg[:, 0:1], ALU.pow).then_inc(rs3_ready, 1)

            def small_load(b):
                for n in range(2):
                    pool.wait_ge(factors_stored[n], 48 * PAIRS_B * (b + 1))
                if b:
                    pool.wait_ge(minv_stored[b - 1], 16)
                for c in range(CPB):
                    for a in range(2):
                        p0 = PAIRS * (2 * c + a)
                        pool.dma_start(msw[p0:p0 + PAIRS, 0],
                                       m_d[CPB * b + c, a, :, :, RANK * a:RANK * (a + 1)].rearrange("r h n -> h r n")
                                       ).then_inc(m_loaded, 16)
                pool.wait_ge(m_inverted, b + 1)
                pool.dma_start(minv_d[2 * CPB * b:2 * CPB * (b + 1)].rearrange("c h i j -> (c h) (i j)"),
                               msw[:, 0].rearrange("p i j -> p (i j)")).then_inc(minv_stored[b], 16)

            for b in range(BATCH):
                small_load(b)

                each_pair(pool, PAIRS_B * b, PAIRS_B * (b + 1), norm3)

        @block.scalar
        def _(act):
            act.wait_ge(ffw_loaded, 32)
            for t in range(FT):
                if t:
                    act.wait_ge(abs_done, t)
                nc.scalar.activation(absw[:, 0:DM], w1n[:, t], ACT.Abs, accum_out=alpha1[:, t:t + 1]).then_inc(abs_done, 1)
            for t in range(KT):
                act.wait_ge(abs_done, FT + t)
                nc.scalar.activation(absw, w2n[:, t], ACT.Abs, accum_out=alpha2[:, t:t + 1]).then_inc(abs_done, 1)
            act.wait_ge(abs_done, FT + KT)
            nc.scalar.activation(w1n, w1n, ACT.Sign).then_inc(sign_done, 1)
            nc.scalar.activation(w2n, w2n, ACT.Sign).then_inc(sign_done, 1)
            nc.scalar.mul(alpha1[:], alpha1[:], 1.0 / DM).then_inc(alpha_done, 1)
            nc.scalar.mul(alpha2[:], alpha2[:], 1.0 / FF).then_inc(alpha_done, 1)
            act.wait_ge(alpha_done, 2)
            act.wait_ge(zeroed, 2)
            for t in range(KT):
                nc.scalar.activation(diag[:, t], ident[:], ACT.Copy, scale=alpha2[:, t:t + 1]).then_inc(diag_done, 1)
            for n in range(8):
                act.wait_ge(sgn_ready, n + 1)
                if n < 4:
                    dst = s1t[:, n // 2, (n % 2) * BANK:(n % 2 + 1) * BANK]
                else:
                    dst = s2t[:, 2 * (n - 4):2 * (n - 3)].rearrange("p t d -> p (t d)")
                nc.scalar.copy(dst, bank[n][:]).then_inc(sgn_copied, 1)
            act.wait_ge(alpha_bcast, 1)
            nc.scalar.copy(alpha2r[:], bank[0][:, 0:DM]).then_inc(alpha_row, 1)

            act.wait_ge(consts_loaded, 48)

            def copy_gc(i, par):
                c = 2 * i + par
                wait(act, gc_stored[par], 16 * i)
                for j in range(2):
                    wait(act, gc_ready, 2 * c + j + 1)
                    nc.scalar.copy(gc[:, par, 4 * j:4 * j + 4].rearrange("p h n -> p (h n)"), bank[4 + j][:]
                                   ).then_inc(gc_copied, 1)

            def project(i, par, lead):
                c = 2 * i + par
                wait(act, xnt_ready, c + 1)
                for t in range(KT):
                    ins = nc.scalar.activation(xnt[:, par, t], bank[0][:, P * t:P * (t + 1)], ACT.Identity,
                                               scale=gain[:, t:t + 1], bias=bias[:, t:t + 1])
                ins.then_inc(xnt_copied, 1)
                if not lead or par == 1:
                    copy_gc(i if par else i - 1, 1 - par)
                for n in range(6):
                    if n == 4:
                        wait(act, q_stored[par], 16 * i)
                    wait(act, kvq_ready, 6 * c + n + 1)
                    if n < 4:
                        dst = kv[:, par, n // 2, (n % 2) * BANK:(n % 2 + 1) * BANK]
                    else:
                        dst = qt[:, par, 4 * (n - 4):4 * (n - 3)].rearrange("p h r -> p (h r)")
                    nc.scalar.copy(dst, bank[1 + n % 3][:]).then_inc(kvq_copied, 1)

            def schur(i, par):
                c = 2 * i + par
                wait(act, t_ready, c + 1)
                nc.scalar.copy(xs[:].rearrange("p h j -> p (h j)"), bank[6][:, 0:PAIRS * HALF]).then_inc(t_copied, 1)
                wait(act, schur_ready, c + 1)
                wait(act, schur_stored[par], 16 * i)
                nc.scalar.copy(sch[:, par].rearrange("p h j -> p (h j)"), bank[7][:, 0:PAIRS * HALF]).then_inc(schur_copied, 1)

            for stage, b in FIRST_PHASE:
                first, last = PAIRS_B * b, PAIRS_B * (b + 1)
                if stage == "project":
                    for par in range(2):
                        project(first, par, True)
                    with act.Fori(first + 1, last) as i:
                        for par in range(2):
                            project(i, par, False)
                    copy_gc(last - 1, 1)
                else:
                    each_pair(act, first, last, schur)

            def chunk(a, b):
                def flat(t):
                    return t.rearrange("p h n -> p (h n)")
                if a:
                    i, par = a
                    c = 2 * i + par
                    wait(act, y_ready, c + 1)
                    nc.scalar.copy(flat(ysb[:]), bank[0][:]).then_inc(y_copied, 1)
                if b:
                    j, q = b
                    d = 2 * j + q
                    wait(act, nz_ready, d + 1)
                    nc.scalar.mul(flat(nz[:]), bank[5][0:2 * RANK, :], -1.0).then_inc(nz_copied, 1)
                if a:
                    wait(act, w2_ready, c + 1)
                    nc.scalar.copy(flat(w2sb[:]), bank[2][:]).then_inc(w2_copied, 1)
                if b:
                    for n in range(2):
                        wait(act, ot_ready, 2 * d + n + 1)
                        nc.scalar.mul(ot[:, 4 * n:4 * n + 4].rearrange("p h r -> p (h r)"), bank[6 + n][:], SCALE
                                      ).then_inc(ot_copied, 1)
                if a:
                    wait(act, w_ready, c + 1)
                    wait(act, wbd_copied, 2 * c)
                    nc.scalar.mul(flat(wt[:]), bank[2][:], -1.0).then_inc(w_copied, 1)
                if b:
                    wait(act, y3t_ready, d + 1)
                    nc.scalar.copy(y3t[:].rearrange("p t r -> p (t r)"), bank[5][:, 0:DM]).then_inc(y3t_copied, 1)
                    for t in range(FT):
                        if t % 4 == 0:
                            wait(act, h_ready, FT * d + t + 4)
                        nc.scalar.activation(ht[:, t], bank[6 + t // 4][:, P * (t % 4):P * (t % 4 + 1)], ACT.Gelu,
                                             scale=alpha1[:, t:t + 1], bias=b1c[:, t:t + 1]).then_inc(h_copied, 1)
                if a:
                    wait(act, factors_stored[par], 48 * i)
                    wait(act, z_ready, c + 1)
                    nc.scalar.copy(zs[:, par], bank[0][0:2 * RANK, :]).then_inc(z_copied, 1)
                    for n in range(2):
                        wait(act, yt_ready, 2 * c + n + 1)
                        nc.scalar.copy(yts[:, par, BANK * n:BANK * (n + 1)], bank[3 + n][0:2 * RANK, :]).then_inc(yt_copied, 1)

            each_pair(act, 0, PAIRS_B, lambda i, par: chunk((i, par), None))
            for b in range(BATCH):
                each_pair(act, PAIRS_B * b, PAIRS_B * (b + 1),
                          lambda i, par: chunk((i + PAIRS_B, par) if b + 1 < BATCH else None, (i, par)))

        @block.vector
        def _(dve):
            V = nc.vector
            dve.wait_ge(zeroed, 4)
            step = [0]

            def link(ins):
                step[0] += 1
                ins.then_inc(ln_step, 1)

            def settle():
                dve.wait_ge(ln_step, step[0])

            def statistics(src, moments, var_eps):
                for k in range(GROUP):
                    link(V.bn_stats(stats[:, k], src[:, k]))
                settle()
                for k in range(GROUP):
                    link(V.bn_aggr(moments[:, k], stats[:, k]))
                settle()
                V.tensor_scalar(var_eps, moments[:, :, 1], LN_EPS, None, ALU.add).then_inc(veps_ready, 1)

            for g in range(NCH // GROUP):
                n = g % 2
                dve.wait_ge(x_loaded[n], 16 * (g // 2 + 1))
                statistics(xg[:, n], mv, veps[:])
                if g >= 2:
                    dve.wait_ge(ln_stored[(g - 2) * GROUP // CPB], 64 if (g - 2) % 2 else 32)
                dve.wait_ge(rstd_ready, 2 * g + 1)
                for k in range(GROUP):
                    link(V.tensor_scalar(lng[:, n, k], xg[:, n, k], mv[:, k, 0:1], rstd[:, k:k + 1],
                                         ALU.subtract, ALU.mult))
                settle()
                statistics(lng[:, n], mv2, veps2[:])
                dve.wait_ge(rstd_ready, 2 * g + 2)
                for k in range(GROUP):
                    link(V.tensor_scalar(hatg[:, n, k], lng[:, n, k], mv2[:, k, 0:1], rstd2[:, k:k + 1],
                                         ALU.subtract, ALU.mult))
                settle()
                V.tensor_tensor(lng[:, n], lng[:, n], xg[:, n], ALU.add).then_inc(hat_ready, 1)

            done = [0]

            def pivot(src, dst, size, strips, count, wait_first):
                n = size
                if wait_first is not None:
                    dve.wait_ge(swept, wait_first)
                V.reciprocal(piv[:], src[:, 0, 0:1]).then_inc(swept, 1)
                dve.wait_ge(swept, count + 1)
                V.tensor_scalar(prow[:, 1:n], src[:, 0, 1:n], piv[:], None, ALU.mult).then_inc(swept, 1)
                V.tensor_scalar(dst[:, 0:n - 1, n - 1], src[:, 0, 1:n], piv[:], None, ALU.mult).then_inc(swept, 1)
                V.tensor_scalar(dst[:, n - 1, n - 1:n], piv[:], -1.0, None, ALU.mult).then_inc(swept, 1)
                dve.wait_ge(swept, count + 2)
                at = 0
                tiles = []
                for r0, r1 in strips:
                    rows, cols = r1 - r0, n - 1 - r0
                    t = outer[:, at:at + rows * cols].rearrange("p (i j) -> p i j", i=rows)
                    at += rows * cols
                    tiles.append(t)
                    V.tensor_tensor(t, src[:, 0, r0 + 1:r1 + 1].unsqueeze(2).broadcast_to([P, rows, cols]),
                                    prow[:, r0 + 1:n].unsqueeze(1).broadcast_to([P, rows, cols]), ALU.mult).then_inc(swept, 1)
                for m, (r0, r1) in enumerate(strips):
                    dve.wait_ge(swept, count + 4 + m + 1)
                    V.tensor_tensor(dst[:, r0:r1, r0:n - 1], src[:, r0 + 1:r1 + 1, r0 + 1:n], tiles[m],
                                    ALU.subtract).then_inc(swept, 1)

            def sweep(k):
                a = work[:, 2 * (k % 2), :].rearrange("p (i j) -> p i j", i=HALF)
                z = work[:, 2 * (k % 2) + 1, :].rearrange("p (i j) -> p i j", i=HALF)
                strips = [(0, 16), (16, 31)]
                per = 4 + 2 * len(strips)
                dve.wait_ge(sweep_loaded[k % 2], 16 * 2 * CPB * (k // 2 + 1))
                dg = work[:, 2 * (k % 2), 0:HALF * HALF:HALF + 1]
                V.tensor_scalar(dg, dg, RIDGE, None, ALU.add).then_inc(swept, 1)
                if k < 2:
                    V.memset(z[:], 0.0).then_inc(swept, 1)
                    done[0] += 1
                done[0] += 1
                base = done[0]
                with dve.Fori(0, HALF // 2) as t:
                    count = t * (2 * per) + base
                    pivot(a, z, HALF, strips, count, count)
                    pivot(z, a, HALF, strips, count + per, count + per)
                done[0] = base + HALF * per
                dve.wait_ge(swept, done[0])
                V.tensor_copy(piv[:], piv[:]).then_inc(inverted, 1)

            for k in range(len(SWEEPS)):
                sweep(k)

            def small_sweep(b):
                a, z = msw[:, 0], msw[:, 1]
                strips = [(0, RANK - 1)]
                per = 4 + 2 * len(strips)
                dve.wait_ge(m_loaded, 16 * 2 * CPB * (b + 1))
                V.memset(z[:], 0.0).then_inc(swept, 1)
                done[0] += 1
                count = done[0]
                for t in range(RANK):
                    src, dst = (a, z) if t % 2 == 0 else (z, a)
                    pivot(src, dst, RANK, strips, count, count)
                    count += per
                done[0] = count
                dve.wait_ge(swept, count)
                for r in range(1, RANK):
                    V.tensor_copy(a[:, r, 0:r], a[:, 0:r, r]).then_inc(swept, 1)
                done[0] += RANK - 1
                dve.wait_ge(swept, done[0])
                V.tensor_copy(piv[:], piv[:]).then_inc(m_inverted, 1)

            def chunk(a, b):
                def flat(t):
                    return t.rearrange("p h n -> p (h n)")
                def banked(n, width):
                    return bank[n][:].rearrange("p (h n) -> p h n", n=width)
                if a:
                    i, par = a
                    c = 2 * i + par
                    wait(dve, g1_ready, c + 1)
                    V.tensor_tensor(rsb[:], banked(1, HD), gct[:, par, :, HD:2 * HD], ALU.add).then_inc(r1_done, 1)
                if b:
                    j, q = b
                    d = 2 * j + q
                    wait(dve, wr_ready, d + 1)
                    for s in range(2):
                        sl = slice(HD * s, HD * (s + 1))
                        V.scalar_tensor_tensor(out=state[sl, q, :, sl], in0=state[sl, 1 - q, :, sl], scalar=DECAY,
                                               in1=banked(5, HD)[sl], op0=ALU.mult, op1=ALU.add).then_inc(state_done, 1)
                if a:
                    wait(dve, g2_ready, c + 1)
                    V.tensor_tensor(r2sb[:], banked(1, HD), gct[:, par, :, HD:2 * HD], ALU.add).then_inc(r2_done, 1)
                if b:
                    wait(dve, wo_ready, d + 1)
                    V.tensor_tensor(x2[:], bank[5][:, 0:DM], resl[:, q], ALU.add).then_inc(x2_done, 1)
                    wait(dve, x2_done, d + 1)
                    V.bn_stats(st3[:], x2[:]).then_inc(ln3_step, 1)
                    wait(dve, ln3_step, 2 * d + 1)
                    V.tensor_tensor(x2b[:], x2[:], b2r[:], ALU.add).then_inc(x2b_done, 1)
                    V.bn_aggr(mv3[:], st3[:]).then_inc(ln3_step, 1)
                    wait(dve, ln3_step, 2 * d + 2)
                    V.tensor_scalar(ve3[:], mv3[:, 1:2], LN_EPS, None, ALU.add).then_inc(ve3_ready, 1)
                if a:
                    wait(dve, w_copied, c + 1)
                    wait(dve, wbdt_ready, 2 * c)
                    for s in range(2):
                        sl = slice(HD * s, HD * (s + 1))
                        V.tensor_copy(wbd[sl, :, sl], wt[sl]).then_inc(wbd_copied, 1)
                    for n in range(2):
                        wait(dve, wbdt_ready, 2 * c + n + 1)
                        V.tensor_copy(flat(wbdt[:, 4 * n:4 * n + 4]), bank[3 + n][:]).then_inc(wbdt_copied, 1)
                if b:
                    wait(dve, rs3_ready, d + 1)
                    V.tensor_scalar(x3[:], x2[:], mv3[:, 0:1], rs3[:], ALU.subtract, ALU.mult).then_inc(x3_ready, 1)
                if a:
                    wait(dve, y2_ready, c + 1)
                    wait(dve, yt_ready, 2 * c)
                    y2 = bank[1][:, 0:PAIRS * RANK].rearrange("p (h n) -> p h n", n=RANK)
                    for s in range(2):
                        sl = slice(HD * s, HD * (s + 1))
                        V.tensor_copy(y2bd[sl, :, RANK * s:RANK * (s + 1)], y2[sl]).then_inc(y2_copied, 1)
                    wait(dve, m_ready, c + 1)
                    wait(dve, factors_stored[par], 48 * i)
                    V.tensor_copy(ms[:, par], bank[1][0:2 * RANK, 256:256 + 2 * RANK * PAIRS]).then_inc(m_copied, 1)
                if b:
                    wait(dve, o_ready, d + 1)
                    V.tensor_tensor(ysc[:], bank[5][:, 0:DM], alpha2r[:], ALU.mult).then_inc(scaled, 1)
                    wait(dve, scaled, d + 1)
                    wait(dve, x2b_done, d + 1)
                    wait(dve, out_stored[q], 16 * j)
                    V.tensor_tensor(yo[:, q], ysc[:], x2b[:], ALU.add).then_inc(o_done, 1)

            dve.wait_ge(alpha_row, 1)
            dve.wait_ge(zeroed, 11)
            dve.wait_ge(b2_loaded, 16)
            each_pair(dve, 0, PAIRS_B, lambda i, par: chunk((i, par), None))
            for b in range(BATCH):
                small_sweep(b)
                if b:
                    dve.wait_ge(ot_ready, 2 * CPB * b)
                    V.memset(state[:, 1], 0.0).then_inc(state_cleared, 1)
                    dve.wait_ge(state_cleared, b)
                each_pair(dve, PAIRS_B * b, PAIRS_B * (b + 1),
                          lambda i, par: chunk((i + PAIRS_B, par) if b + 1 < BATCH else None, (i, par)))

        @block.tensor
        def _(pe):
            mm = nc.tensor.matmul
            pe.wait_ge(zeroed, 2)
            pe.wait_ge(sign_done, 2)
            for n in range(8):
                for t in range(4):
                    if n < 4:
                        src = w1n[:, 4 * (n % 2) + t, P * (n // 2):P * (n // 2 + 1)]
                    else:
                        src = w2n[:, t % 2, P * (2 * (n - 4) + t // 2):P * (2 * (n - 4) + t // 2 + 1)]
                    ins = nc.tensor.transpose(bank[n][:, P * t:P * (t + 1)], src, ident[:])
                ins.then_inc(sgn_ready, 1)
            pe.wait_ge(diag_done, 2)
            pe.wait_ge(zeroed, 4)
            pe.wait_ge(sgn_copied, 8)
            mm(bank[0][:, 0:DM], ones[:], diag[:].rearrange("p t d -> p (t d)"), start=True, stop=True).then_inc(alpha_bcast, 1)
            pe.wait_ge(alpha_row, 1)
            pe.wait_ge(qkv_loaded, 64)

            def gram(i, par):
                c = 2 * i + par
                wait(pe, kvq_copied, 6 * c + 4)
                for j in range(2):
                    wait(pe, gc_copied, 2 * c + j - 1)
                    for h in range(8 * j, 8 * j + 8):
                        cols = slice(HD * h, HD * (h + 1))
                        lo = HD * (h % 2)
                        at = 2 * HD * (h // 2 % 4)
                        ins = mm(bank[4 + j][lo:lo + HD, at:at + 2 * HD], kv[:, par, 0, cols], kv[:, par, :, cols],
                                 start=True, stop=True)
                    ins.then_inc(gc_ready, 1)

            def project(i, par, lead):
                c = 2 * i + par
                wait(pe, xhat_loaded[par], 16 * (i + 1))
                wait(pe, xnt_copied, c)
                for t in range(KT):
                    ins = nc.tensor.transpose(bank[0][:, P * t:P * (t + 1)], xh[:, par, P * t:P * (t + 1)], ident[:])
                ins.then_inc(xnt_ready, 1)
                if not lead or par == 1:
                    gram(i if par else i - 1, 1 - par)
                wait(pe, xnt_copied, c + 1)
                for n in range(6):
                    wait(pe, kvq_copied, 6 * c + n - 2)
                    dst = bank[1 + n % 3]
                    if n < 4:
                        for t in range(KT):
                            ins = mm(dst[:], xnt[:, par, t], wqkv[:, n // 2, t, (n % 2) * BANK:(n % 2 + 1) * BANK],
                                     start=t == 0, stop=t == KT - 1)
                    else:
                        for h in range(4):
                            cols = slice(P * (4 * (n - 4) + h), P * (4 * (n - 4) + h + 1))
                            for t in range(KT):
                                ins = mm(dst[:, P * h:P * (h + 1)], wqkv[:, 2, t, cols], xnt[:, par, t],
                                         start=t == 0, stop=t == KT - 1)
                    ins.then_inc(kvq_ready, 1)

            def schur(i, par):
                c = 2 * i + par
                wait(pe, blocks_loaded[par], 80 * (i + 1))
                wait(pe, t_copied, c)
                for h in range(PAIRS):
                    ins = mm(bank[6][:, HALF * h:HALF * (h + 1)], pbd[:, par, h], gct[:, par, h, HALF:HD], start=True, stop=True)
                ins.then_inc(t_ready, 1)
                wait(pe, schur_copied, c)
                mm(bank[7][:, 0:HALF * PAIRS], ident[:], gct[:, par, :, HALF:HD], start=True, stop=False,
                   skip_group_check=True)
                wait(pe, t_copied, c + 1)
                for h in range(PAIRS):
                    ins = mm(bank[7][:, HALF * h:HALF * (h + 1)], gbd[:, par, h], xs[:, h], start=False, stop=h == PAIRS - 1,
                             skip_group_check=True)
                ins.then_inc(schur_ready, 1)

            for stage, b in FIRST_PHASE:
                first, last = PAIRS_B * b, PAIRS_B * (b + 1)
                if stage == "project":
                    for par in range(2):
                        project(first, par, True)
                    with pe.Fori(first + 1, last) as i:
                        for par in range(2):
                            project(i, par, False)
                    gram(last - 1, 1)
                else:
                    each_pair(pe, first, last, schur)

            pe.wait_ge(gc_copied, 2 * NCH)
            pe.wait_ge(kvq_copied, 6 * NCH)
            pe.wait_ge(t_copied, NCH)
            pe.wait_ge(schur_copied, NCH)

            def chunk(a, b):
                def at(n, h, w=HD):
                    return bank[n][:, w * h:w * (h + 1)]
                if a:
                    i, par = a
                    c = 2 * i + par
                    wait(pe, solve_loaded[par], 112 * (i + 1))
                    wait(pe, z_copied, c)
                    for h in range(PAIRS):
                        ins = mm(at(0, h), pbd[:, par, h], gct[:, par, h, HD:2 * HD], start=True, stop=True)
                    ins.then_inc(y_ready, 1)
                if b:
                    j, q = b
                    d = 2 * j + q
                    wait(pe, apply_loaded[q], 96 * (j + 1))
                    wait(pe, scaled, d)
                    for h in range(PAIRS):
                        m = mbd[:, q].rearrange("p h n -> p (h n)") if h == 0 else mbd[:, q, h]
                        ins = mm(bank[5][0:m.shape[1], HD * h:HD * (h + 1)], m, zl[:, q, h], start=True, stop=True)
                    ins.then_inc(nz_ready, 1)
                if a:
                    wait(pe, y_copied, c + 1)
                    wait(pe, m_copied, c)
                    for h in range(PAIRS):
                        ins = mm(at(1, h), gbd[:, par, h], ysb[:, h], start=True, stop=True)
                    ins.then_inc(g1_ready, 1)
                if b:
                    wait(pe, nz_copied, d + 1)
                    for h in range(PAIRS):
                        ins = mm(at(5, h), ytl[:, q, h], nz[:, h], start=True, stop=True)
                    ins.then_inc(wr_ready, 1)
                if a:
                    wait(pe, r1_done, c + 1)
                    wait(pe, w_copied, c)
                    for h in range(PAIRS):
                        ins = mm(at(2, h), sbd[:, par, h], rsb[:, h], start=h == 0, stop=False, skip_group_check=True)
                    ins.then_inc(w2_ready, 1)
                if b:
                    wait(pe, state_done, 2 * (d + 1))
                    for n in range(2):
                        wait(pe, h_copied, FT * d - 4 * (1 - n))
                        for h in range(4 * n, 4 * n + 4):
                            ins = mm(bank[6 + n][:, P * (h % 4):P * (h % 4 + 1)], state[:, q, h], qt[:, q, h],
                                     start=True, stop=True)
                        ins.then_inc(ot_ready, 1)
                if a:
                    wait(pe, w2_copied, c + 1)
                    for h in range(PAIRS):
                        ins = mm(at(1, h), gbd[:, par, h], w2sb[:, h], start=True, stop=True)
                    ins.then_inc(g2_ready, 1)
                if b:
                    for h in range(PAIRS):
                        wait(pe, ot_copied, 2 * d + h // 4 + 1)
                        ins = mm(bank[5][:, 0:DM], ot[:, h], wo[:, h], start=h == 0, stop=h == PAIRS - 1)
                    ins.then_inc(wo_ready, 1)
                if a:
                    wait(pe, r2_done, c + 1)
                    for h in range(PAIRS):
                        ins = mm(at(2, h), pbd[:, par, h], r2sb[:, h], start=False, stop=h == PAIRS - 1, skip_group_check=True)
                    ins.then_inc(w_ready, 1)
                    wait(pe, wbd_copied, 2 * (c + 1))
                    wait(pe, yt_copied, 2 * c)
                    for n in range(2):
                        for h in range(4):
                            ins = nc.tensor.transpose(at(3 + n, h, P), wbd[:, 4 * n + h], ident[:])
                        ins.then_inc(wbdt_ready, 1)
                if b:
                    wait(pe, x3_ready, d + 1)
                    for t in range(KT):
                        ins = nc.tensor.transpose(bank[5][:, P * t:P * (t + 1)], x3[:, P * t:P * (t + 1)], ident[:])
                    ins.then_inc(y3t_ready, 1)
                if a:
                    for h in range(PAIRS):
                        wait(pe, wbdt_copied, 2 * c + h // 4 + 1)
                        ins = mm(at(1, h, RANK), wbdt[:, h], wt[:, h, 0:RANK], start=True, stop=True)
                    ins.then_inc(y2_ready, 1)
                if b:
                    wait(pe, y3t_copied, d + 1)
                    for t in range(FT):
                        for k in range(KT):
                            ins = mm(bank[6 + t // 4][:, P * (t % 4):P * (t % 4 + 1)], s1t[:, k, P * t:P * (t + 1)], y3t[:, k],
                                     start=k == 0, stop=k == KT - 1)
                        ins.then_inc(h_ready, 1)
                if a:
                    wait(pe, y2_copied, 2 * (c + 1))
                    for h in range(PAIRS):
                        ins = mm(bank[0][0:2 * RANK, HD * h:HD * (h + 1)], y2bd[:, h], wt[:, h], start=True, stop=True)
                    ins.then_inc(z_ready, 1)
                    for h in range(PAIRS):
                        o = 256 + 2 * RANK * h
                        ins = mm(bank[1][0:2 * RANK, o:o + 2 * RANK], y2bd[:, h], y2bd[:, h], start=True, stop=True)
                    ins.then_inc(m_ready, 1)
                    for n in range(2):
                        for h in range(4):
                            ins = nc.tensor.transpose(bank[3 + n][0:2 * RANK, P * h:P * (h + 1)], y2bd[:, 4 * n + h], ident[:])
                        ins.then_inc(yt_ready, 1)
                if b:
                    for t in range(FT):
                        wait(pe, h_copied, FT * d + t + 1)
                        ins = mm(bank[5][:, 0:DM], ht[:, t], s2t[:, t], start=t == 0, stop=t == FT - 1)
                    ins.then_inc(o_ready, 1)

            each_pair(pe, 0, PAIRS_B, lambda i, par: chunk((i, par), None))
            for b in range(BATCH):
                each_pair(pe, PAIRS_B * b, PAIRS_B * (b + 1),
                          lambda i, par: chunk((i + PAIRS_B, par) if b + 1 < BATCH else None, (i, par)))


_INS = ["L0_attn_x", "L0_attn_ln_g", "L0_attn_ln_b", "L0_attn_Wq", "L0_attn_Wk", "L0_attn_Wv", "L0_attn_Wo",
        "L0_ffn_w1", "L0_ffn_b1", "L0_ffn_w2", "L0_ffn_b2"]


def kernel(**inputs):
    import numpy as _np
    import concourse.bacc as _bacc
    from concourse import mybir as _mybir
    from concourse.bass_utils import run_bass_kernel_spmd as _run

    nc = _bacc.Bacc("TRN2", target_bir_lowering=False, num_devices=1)
    arrays, args = {}, []
    for name in _INS:
        a = _np.ascontiguousarray(inputs[name])
        arrays[f"in_{name}_dram"] = a
        args.append(nc.dram_tensor(f"in_{name}_dram", a.shape, _mybir.dt.from_np(a.dtype), kind="ExternalInput").ap())
    args.append(nc.dram_tensor("out_0_dram", (BATCH, SEQ, DM), _mybir.dt.float32, kind="ExternalOutput").ap())
    build(nc, *args)
    r = _run(nc, [arrays], core_ids=[0])
    return r.results[0]["out_0_dram"]
```

```python
from contextlib import ExitStack

import concourse.bass as bass
from concourse import mybir

P = 128
ALU = mybir.AluOpType
ACT = mybir.ActivationFunctionType
F32 = mybir.dt.float32

BATCH, SEQ, DM = 4, 1024, 256
HEADS, HD, RANK = 16, 64, 8
CHUNK = P
CPB = SEQ // CHUNK
NCH = BATCH * CPB
PAIRS = HEADS // 2
KT = DM // P
HALF = HD // 2
FF = 1024
FT = FF // P
BANK = 512

RIDGE, LN_EPS, SCALE, DECAY = 1e-4, 1e-5, 0.125, 0.9
GROUP = 4

SWEEPS = [(0, 0), (0, 1), (1, 0), (0, 2), (1, 1), (0, 3), (1, 2), (1, 3)]
PROGRAM = [("project", 0), ("sweep", 0), ("project", 1), ("project", 2), ("schur", 0), ("sweep", 1),
           ("project", 3), ("schur", 1), ("sweep", 2), ("fused", 0, None, 3), ("schur", 2), ("sweep", 4),
           ("small", 0), ("fused", 1, 0, 5), ("schur", 3), ("sweep", 6), ("small", 1), ("fused", 2, 1, 7),
           ("small", 2), ("fused", 3, 2, None), ("small", 3), ("fused", None, 3, None)]


def build(nc, x, ln_g, ln_b, Wq, Wk, Wv, Wo, w1, b1, w2, b2, out):
    x_rows = x.rearrange("b s d -> (b s) d")
    x_groups = x_rows.rearrange("(g k p) d -> g p k d", p=P, k=GROUP)
    out_chunks = out.rearrange("b s d -> (b s) d").rearrange("(c p) d -> c p d", p=P)

    def scratch(name, shape):
        return nc.dram_tensor(name, shape, F32, kind="Internal").ap()

    xhat_d = scratch("xhat_d", [NCH, P, DM])
    res_d = scratch("res_d", [NCH, P, DM])
    gc_d = scratch("gc_d", [2 * NCH, PAIRS, HD, 2 * HD])
    q_d = scratch("q_d", [NCH, P, PAIRS, P])
    schur_d = scratch("schur_d", [2 * NCH, PAIRS, HALF, HALF])
    inv_d = [scratch(f"inv{k}_d", [2 * NCH, PAIRS, HALF, HALF]) for k in range(2)]
    z_d = scratch("z_d", [NCH, 2 * RANK, PAIRS * HD])
    yt_d = scratch("yt_d", [NCH, 2 * RANK, PAIRS * P])
    m_d = scratch("m_d", [2 * NCH, PAIRS, RANK, RANK])
    minv_d = scratch("minv_d", [2 * NCH, PAIRS, RANK, RANK])

    with ExitStack() as ctx:
        def sb(name, shape, dt=F32):
            return ctx.enter_context(nc.sbuf_tensor(name, shape, dt))

        def sem(name):
            return ctx.enter_context(nc.semaphore(name))

        bank = [ctx.enter_context(nc.psum_tensor(f"bank{n}", [P, BANK], F32)) for n in range(8)]

        wqkv = sb("wqkv", [P, 3, KT, HEADS * HD])
        wo = sb("wo", [P, PAIRS, DM])
        s1t = sb("s1t", [P, KT, FF])
        s2t = sb("s2t", [P, FT, DM])
        ident = sb("ident", [P, P])
        ones = sb("ones", [P, P])
        diag = sb("diag", [P, KT, P])
        gain = sb("gain", [P, KT])
        bias = sb("bias", [P, KT])
        b1c = sb("b1c", [P, FT])
        b2r = sb("b2r", [P, DM])
        alpha1 = sb("alpha1", [P, FT])
        alpha2 = sb("alpha2", [P, KT])
        alpha2r = sb("alpha2r", [P, DM])
        half_neg = sb("half_neg", [P, GROUP])
        work = sb("work", [P, 4, HALF * HALF])
        w1n = work[:, 0:2, :].rearrange("p a n -> p (a n)").rearrange("p (t d) -> p t d", d=DM)
        w2n = work[:, 2:4, :]
        early = sb("early", [P, 3 * 2 * GROUP * DM])
        xg, lng, hatg = (early[:, 2 * GROUP * DM * n:2 * GROUP * DM * (n + 1)].rearrange(
            "p (a k d) -> p a k d", a=2, k=GROUP) for n in range(3))
        stats = sb("stats", [P, GROUP, 6])
        mv = sb("mv", [P, GROUP, 2])
        mv2 = sb("mv2", [P, GROUP, 2])
        veps = sb("veps", [P, GROUP])
        veps2 = sb("veps2", [P, GROUP])
        rstd = sb("rstd", [P, GROUP])
        rstd2 = sb("rstd2", [P, GROUP])
        xh = sb("xh", [P, 2, DM])
        xnt = sb("xnt", [P, 2, KT, P])
        kv = sb("kv", [P, 2, 2, HEADS * HD])
        absw = kv[:, 0, 0, :]
        qt = sb("qt", [P, 2, PAIRS, P])
        gc = sb("gc", [P, 2, PAIRS, 2 * HD])
        gct = sb("gct", [P, 2, PAIRS, 2 * HD])
        gbd = sb("gbd", [P, 2, PAIRS, P])
        pbd = sb("pbd", [P, 2, PAIRS, P])
        sbd = sb("sbd", [P, 2, PAIRS, P])
        xs = sb("xs", [P, PAIRS, HALF])
        sch = sb("sch", [P, 2, PAIRS, HALF])
        upper = sb("upper", [P, HALF, HALF])
        lower = sb("lower", [P, HALF, HALF])
        piv = sb("piv", [P, 1])
        prow = sb("prow", [P, HALF])
        outer = sb("outer", [P, 16 * 31 + 15 * 15])
        used = [0]

        def late(*dims):
            size = 1
            for n in dims:
                size *= n
            part = early[:, used[0]:used[0] + size]
            used[0] += size
            assert used[0] <= early.shape[1]
            return part.rearrange("p (a b) -> p a b", a=dims[0]) if len(dims) == 2 else part

        ysb, rsb, w2sb, r2sb, wt = (late(PAIRS, HD) for _ in range(5))
        wbd = sb("wbd", [P, PAIRS, P])
        wbdt = late(PAIRS, P)
        y2bd = sb("y2bd", [P, PAIRS, 2 * RANK])
        zs = kv[0:2 * RANK, 1, 0, :].rearrange("p (a n) -> p a n", a=2)
        yts = gc[0:2 * RANK].rearrange("p a h n -> p a (h n)")
        ms = sb("ms", [2 * RANK, 2, PAIRS * 2 * RANK])
        msw = sb("msw", [P, 2, RANK, RANK])
        zl = sb("zl", [2 * RANK, 2, PAIRS, HD])
        ytl = sb("ytl", [2 * RANK, 2, PAIRS, P])
        mbd = sb("mbd", [2 * RANK, 2, PAIRS, 2 * RANK])
        nz = sb("nz", [2 * RANK, PAIRS, HD])
        state = sb("state", [P, 2, PAIRS, P])
        ot = kv[:, 0, 0, :].rearrange("p (h r) -> p h r", h=PAIRS)
        ht = kv[:, 0, 1, :].rearrange("p (t r) -> p t r", t=FT)
        resl = late(2, DM)
        x2, x2b, x3, ysc = (late(DM) for _ in range(4))
        st3 = sb("st3", [P, 6])
        mv3 = sb("mv3", [P, 2])
        ve3 = sb("ve3", [P, 1])
        rs3 = sb("rs3", [P, 1])
        y3t = late(KT, P)
        yo = late(2, DM)

        consts_loaded = sem("consts_loaded")
        qkv_loaded = sem("qkv_loaded")
        ffw_loaded = sem("ffw_loaded")
        b2_loaded = sem("b2_loaded")
        zeroed = sem("zeroed")
        abs_done = sem("abs_done")
        alpha_done = sem("alpha_done")
        sign_done = sem("sign_done")
        diag_done = sem("diag_done")
        sgn_ready = sem("sgn_ready")
        sgn_copied = sem("sgn_copied")
        alpha_bcast = sem("alpha_bcast")
        alpha_row = sem("alpha_row")
        x_loaded = [sem(f"x_loaded{n}") for n in range(2)]
        ln_step = sem("ln_step")
        veps_ready = sem("veps_ready")
        rstd_ready = sem("rstd_ready")
        hat_ready = sem("hat_ready")
        ln_stored = [sem(f"ln_stored{n}") for n in range(BATCH)]
        xhat_loaded = [sem(f"xhat_loaded{n}") for n in range(2)]
        xnt_ready = sem("xnt_ready")
        xnt_copied = sem("xnt_copied")
        kvq_ready = sem("kvq_ready")
        kvq_copied = sem("kvq_copied")
        gc_ready = sem("gc_ready")
        gc_copied = sem("gc_copied")
        gc_stored = [sem(f"gc_stored{n}") for n in range(2)]
        q_stored = [sem(f"q_stored{n}") for n in range(2)]
        blocks_loaded = [sem(f"blocks_loaded{n}") for n in range(2)]
        t_ready = sem("t_ready")
        t_copied = sem("t_copied")
        schur_ready = sem("schur_ready")
        schur_copied = sem("schur_copied")
        schur_stored = [sem(f"schur_stored{n}") for n in range(2)]
        sweep_loaded = [sem(f"sweep_loaded{n}") for n in range(2)]
        swept = sem("swept")
        inverted = sem("inverted")
        mirrored = sem("mirrored")
        inv_stored = [sem(f"inv_stored{k}") for k in range(len(SWEEPS))]
        solve_loaded = [sem(f"solve_loaded{n}") for n in range(2)]
        y_ready, y_copied = sem("y_ready"), sem("y_copied")
        g1_ready, r1_done = sem("g1_ready"), sem("r1_done")
        w2_ready, w2_copied = sem("w2_ready"), sem("w2_copied")
        g2_ready, r2_done = sem("g2_ready"), sem("r2_done")
        w_ready, w_copied = sem("w_ready"), sem("w_copied")
        wbd_copied = sem("wbd_copied")
        wbdt_ready, wbdt_copied = sem("wbdt_ready"), sem("wbdt_copied")
        y2_ready, y2_copied = sem("y2_ready"), sem("y2_copied")
        z_ready, z_copied = sem("z_ready"), sem("z_copied")
        m_ready, m_copied = sem("m_ready"), sem("m_copied")
        yt_ready, yt_copied = sem("yt_ready"), sem("yt_copied")
        factors_stored = [sem(f"factors_stored{n}") for n in range(2)]
        m_loaded = sem("m_loaded")
        m_inverted = sem("m_inverted")
        minv_stored = [sem(f"minv_stored{n}") for n in range(BATCH)]
        apply_loaded = [sem(f"apply_loaded{n}") for n in range(2)]
        nz_ready, nz_copied = sem("nz_ready"), sem("nz_copied")
        wr_ready = sem("wr_ready")
        state_cleared = sem("state_cleared")
        state_done = sem("state_done")
        ot_ready, ot_copied = sem("ot_ready"), sem("ot_copied")
        wo_ready = sem("wo_ready")
        x2_done = sem("x2_done")
        x2b_done = sem("x2b_done")
        ln3_step = sem("ln3_step")
        ve3_ready, rs3_ready, x3_ready = sem("ve3_ready"), sem("rs3_ready"), sem("x3_ready")
        y3t_ready, y3t_copied = sem("y3t_ready"), sem("y3t_copied")
        h_ready, h_copied = sem("h_ready"), sem("h_copied")
        o_ready, scaled, o_done = sem("o_ready"), sem("scaled"), sem("o_done")
        out_stored = [sem(f"out_stored{n}") for n in range(2)]

        block = ctx.enter_context(nc.Block())

        PAIRS_B = CPB // 2

        def wait(eng, s, value):
            if isinstance(value, int) and value <= 0:
                return
            eng.wait_ge(s, value)

        def each_pair(eng, first, last, body):
            if first == 0:
                for par in range(2):
                    body(0, par)
                first = 1
            with eng.Fori(first, last) as i:
                for par in range(2):
                    body(i, par)

        def fused_pairs(eng, a, b, chunk):
            lead = b if b is not None else a
            shift = PAIRS_B * (a - lead) if a is not None else 0
            each_pair(eng, PAIRS_B * lead, PAIRS_B * (lead + 1),
                      lambda i, par: chunk((i + shift, par) if a is not None else None,
                                           (i, par) if b is not None else None))

        @block.sync
        def _(sp):
            sp.dma_start(gain[:], ln_g.rearrange("(t p) -> p t", p=P), allow_slow_non_contiguous=True).then_inc(consts_loaded, 16)
            sp.dma_start(bias[:], ln_b.rearrange("(t p) -> p t", p=P), allow_slow_non_contiguous=True).then_inc(consts_loaded, 16)
            sp.dma_start(b1c[:], b1.rearrange("(t p) -> p t", p=P), allow_slow_non_contiguous=True).then_inc(consts_loaded, 16)
            sp.dma_start(w1n, w1.rearrange("(t p) d -> p t d", p=P)).then_inc(ffw_loaded, 16)
            sp.dma_start(w2n, w2.rearrange("(t p) h -> p t h", p=P)).then_inc(ffw_loaded, 16)
            for n, w in enumerate((Wk, Wv, Wq)):
                sp.dma_start(wqkv[:, n], w.rearrange("(t p) h -> p t h", p=P)).then_inc(qkv_loaded, 16)
            sp.dma_start(wo[:], Wo.rearrange("(h p) d -> p h d", p=P)).then_inc(qkv_loaded, 16)
            sp.dma_start(b2r[:], b2.rearrange("(a d) -> a d", a=1).broadcast_to([P, DM])).then_inc(b2_loaded, 16)

            def store_gc(i, par):
                wait(sp, gc_copied, 2 * (2 * i + par + 1))
                for a in range(2):
                    sp.dma_start(gc_d[bass.ds(2 * (2 * i + par) + a, 1)].rearrange("a h r n -> (a r) h n"),
                                 gc[HD * a:HD * (a + 1), par]).then_inc(gc_stored[par], 16)

            def store_q(i, par):
                wait(sp, kvq_copied, 6 * (2 * i + par + 1))
                sp.dma_start(q_d[bass.ds(2 * i + par, 1)].rearrange("a p h r -> (a p) h r"),
                             qt[:, par]).then_inc(q_stored[par], 16)

            def project(i, par, lead):
                c = 2 * i + par
                wait(sp, xnt_ready, c - 1)
                sp.dma_start(xh[:, par], xhat_d[bass.ds(c, 1)].rearrange("a p d -> (a p) d")).then_inc(xhat_loaded[par], 16)
                if not lead or par == 1:
                    if not lead:
                        store_gc(i - 1, par)
                    store_q(i if par else i - 1, 1 - par)

            def blocks(i, par, which, halves, s):
                dst = (pbd, sbd)[which]
                for a in range(2):
                    lo = HD * a + HALF * which
                    sp.dma_start(dst[lo:lo + HALF, par, :, lo:lo + HALF],
                                 inv_d[which][bass.ds(2 * (2 * i + par) + a, 1)].rearrange("a h i j -> (a i) h j")
                                 ).then_inc(s, 16)

            def load_gram(i, par, s):
                c2 = 2 * (2 * i + par)
                for a in range(2):
                    sl = slice(HD * a, HD * (a + 1))
                    sp.dma_start(gct[sl, par], gc_d[bass.ds(c2 + a, 1)].rearrange("a h r n -> (a r) h n")).then_inc(s, 16)
                    sp.dma_start(gbd[sl, par, :, sl],
                                 gc_d[bass.ds(c2 + a, 1), :, :, 0:HD].rearrange("a h r n -> (a r) h n")).then_inc(s, 16)

            def store_schur(i, par):
                wait(sp, schur_copied, 2 * i + par + 1)
                for a in range(2):
                    sp.dma_start(schur_d[bass.ds(2 * (2 * i + par) + a, 1)].rearrange("a h r n -> (a r) h n"),
                                 sch[HD * a + HALF:HD * (a + 1), par]).then_inc(schur_stored[par], 16)

            def schur(i, par, lead):
                wait(sp, schur_ready, 2 * i + par - 1)
                load_gram(i, par, blocks_loaded[par])
                blocks(i, par, 0, None, blocks_loaded[par])
                if not lead or par == 1:
                    store_schur(i if par else i - 1, 1 - par)

            def solve(i, par):
                c = 2 * i + par
                wait(sp, w_ready, c - 1)
                wait(sp, r2_done, c - 1)
                load_gram(i, par, solve_loaded[par])
                blocks(i, par, 0, None, solve_loaded[par])
                blocks(i, par, 1, None, solve_loaded[par])

            def store_factors(i, par):
                c = 2 * i + par
                wait(sp, z_copied, c + 1)
                sp.dma_start(z_d[bass.ds(c, 1)].rearrange("a r n -> (a r) n"), zs[:, par]).then_inc(factors_stored[par], 16)
                wait(sp, m_copied, c + 1)
                for a in range(2):
                    sl = slice(RANK * a, RANK * (a + 1))
                    sp.dma_start(m_d[bass.ds(2 * c + a, 1)].rearrange("a h r n -> (a r) h n"),
                                 ms[sl, par].rearrange("r (h n) -> r h n", h=PAIRS)[:, :, sl]).then_inc(factors_stored[par], 16)
                wait(sp, yt_copied, 2 * (c + 1))
                sp.dma_start(yt_d[bass.ds(c, 1)].rearrange("a r n -> (a r) n"), yts[:, par]).then_inc(factors_stored[par], 16)

            def load_apply(i, par):
                c = 2 * i + par
                wait(sp, ot_ready, 2 * (c - 1))
                wait(sp, x2_done, c - 1)
                s = apply_loaded[par]
                sp.dma_start(zl[:, par], z_d[bass.ds(c, 1)].rearrange("a r (h n) -> (a r) h n", h=PAIRS)).then_inc(s, 16)
                sp.dma_start(ytl[:, par], yt_d[bass.ds(c, 1)].rearrange("a r (h n) -> (a r) h n", h=PAIRS)).then_inc(s, 16)
                for a in range(2):
                    lo = RANK * a
                    sp.dma_start(mbd[lo:lo + RANK, par, :, lo:lo + RANK],
                                 minv_d[bass.ds(2 * c + a, 1)].rearrange("a h i j -> (a i) h j")).then_inc(s, 16)
                sp.dma_start(qt[:, par], q_d[bass.ds(c, 1)].rearrange("a p h r -> (a p) h r")).then_inc(s, 16)
                sp.dma_start(resl[:, par], res_d[bass.ds(c, 1)].rearrange("a p d -> (a p) d")).then_inc(s, 16)

            def store_out(i, par):
                c = 2 * i + par
                wait(sp, o_done, c + 1)
                sp.dma_start(out_chunks[bass.ds(c, 1)].rearrange("a p d -> (a p) d"), yo[:, par]).then_inc(out_stored[par], 16)

            def project_all(b):
                first, last = PAIRS_B * b, PAIRS_B * (b + 1)
                sp.wait_ge(ln_stored[b], 64)
                for par in range(2):
                    project(first, par, True)
                with sp.Fori(first + 1, last) as i:
                    for par in range(2):
                        project(i, par, False)
                store_gc(last - 1, 0)
                store_q(last - 1, 1)
                store_gc(last - 1, 1)

            def schur_all(b, solved):
                first, last = PAIRS_B * b, PAIRS_B * (b + 1)
                for n in range(2):
                    sp.wait_ge(gc_stored[n], 32 * last)
                sp.wait_ge(inv_stored[SWEEPS.index((0, b))], 16)
                wait(sp, w_ready, solved)
                wait(sp, r2_done, solved)
                for par in range(2):
                    schur(first, par, True)
                with sp.Fori(first + 1, last) as i:
                    for par in range(2):
                        schur(i, par, False)
                store_schur(last - 1, 1)

            def fused(a, b, formed):
                shift = PAIRS_B * (a - b) if a is not None and b is not None else 0
                lead = PAIRS_B * (b if b is not None else a)
                if a is not None:
                    sp.wait_ge(schur_ready, formed)
                    for k in range(2):
                        sp.wait_ge(inv_stored[SWEEPS.index((k, a))], 16)

                def loads(i, par):
                    if a is not None:
                        solve(i + shift, par)
                    if b is not None:
                        if isinstance(i, int) and (i, par) == (lead, 0):
                            sp.wait_ge(minv_stored[b], 16)
                        load_apply(i, par)

                def stores(i, par):
                    if a is not None:
                        store_factors(i + shift, par)
                    if b is not None:
                        store_out(i, par)

                loads(lead, 0)
                loads(lead, 1)
                stores(lead, 0)
                with sp.Fori(lead + 1, lead + PAIRS_B) as i:
                    loads(i, 0)
                    stores(i - 1, 1)
                    loads(i, 1)
                    stores(i, 0)
                stores(lead + PAIRS_B - 1, 1)

            sp.wait_ge(zeroed, 11)
            formed = solved = 0
            for stage, *at in PROGRAM:
                if stage == "project":
                    project_all(*at)
                elif stage == "schur":
                    schur_all(*at, solved)
                    formed += CPB
                elif stage == "fused":
                    if at[1] == 0:
                        for n in range(2):
                            sp.wait_ge(q_stored[n], 16 * NCH // 2)
                    fused(at[0], at[1], formed)
                    if at[0] is not None:
                        solved += CPB
            for n in range(2):
                sp.wait_ge(out_stored[n], 16 * NCH // 2)
                sp.wait_ge(factors_stored[n], 64 * NCH // 2)

        @block.gpsimd
        def _(pool):
            nc.gpsimd.memset(ident[:], 0.0).then_inc(zeroed, 1)
            pool.wait_ge(zeroed, 1)
            nc.gpsimd.affine_select(out=ident[:], in_=ident[:], compare_op=ALU.not_equal, fill=1.0, base=0,
                                    pattern=[[-1, P]], channel_multiplier=1).then_inc(zeroed, 1)
            nc.gpsimd.memset(half_neg[:], -0.5).then_inc(zeroed, 1)
            nc.gpsimd.memset(ones[:], 1.0).then_inc(zeroed, 1)
            for g in range(2):
                pool.dma_start(xg[:, g], x_groups[g]).then_inc(x_loaded[g], 16)
            for t in (gbd, pbd, sbd, wbd, y2bd, mbd, state):
                nc.gpsimd.memset(t[:], 0.0).then_inc(zeroed, 1)

            for g in range(NCH // GROUP):
                pool.wait_ge(veps_ready, 2 * g + 1)
                nc.gpsimd.tensor_tensor(rstd[:], veps[:], half_neg[:], ALU.pow).then_inc(rstd_ready, 1)
                pool.wait_ge(veps_ready, 2 * g + 2)
                nc.gpsimd.tensor_tensor(rstd2[:], veps2[:], half_neg[:], ALU.pow).then_inc(rstd_ready, 1)
                pool.wait_ge(hat_ready, g + 1)
                b = g * GROUP // CPB
                chunks = slice(g * GROUP, (g + 1) * GROUP)
                pool.dma_start(xhat_d[chunks].rearrange("k p d -> p k d"), hatg[:, g % 2]).then_inc(ln_stored[b], 16)
                pool.dma_start(res_d[chunks].rearrange("k p d -> p k d"), lng[:, g % 2]).then_inc(ln_stored[b], 16)
                if g + 2 < NCH // GROUP:
                    pool.dma_start(xg[:, g % 2], x_groups[g + 2]).then_inc(x_loaded[g % 2], 16)

            def load(k):
                which, b = SWEEPS[k]
                chunks = slice(2 * CPB * b, 2 * CPB * (b + 1))
                for n in range(2):
                    pool.wait_ge((gc_stored, schur_stored)[which][n], 32 * PAIRS_B * (b + 1))
                if k >= 2:
                    pool.wait_ge(mirrored, 3 * (k - 1))
                if which == 0:
                    src = gc_d[chunks, :, 0:HALF, 0:HALF]
                else:
                    src = schur_d[chunks]
                pool.dma_start(work[:, 2 * (k % 2), :].rearrange("p (i j) -> p i j", i=HALF),
                               src.rearrange("c h i j -> (c h) i j")).then_inc(sweep_loaded[k % 2], 16)

            def finish(k):
                which, b = SWEEPS[k]
                pool.wait_ge(inverted, k + 1)
                if k >= 1:
                    pool.wait_ge(inv_stored[k - 1], 16)
                src = work[:, 2 * (k % 2), :].rearrange("p (i j) -> p i j", i=HALF)
                nc.gpsimd.affine_select(out=upper[:], in_=src, compare_op=ALU.is_ge, fill=0.0, base=0,
                                        pattern=[[-1, HALF], [1, HALF]], channel_multiplier=0).then_inc(mirrored, 1)
                nc.gpsimd.affine_select(out=lower[:], in_=src.rearrange("p i j -> p j i"), compare_op=ALU.is_gt,
                                        fill=0.0, base=0, pattern=[[1, HALF], [-1, HALF]],
                                        channel_multiplier=0).then_inc(mirrored, 1)
                pool.wait_ge(mirrored, 3 * k + 2)
                nc.gpsimd.tensor_tensor(upper[:], upper[:], lower[:], ALU.add).then_inc(mirrored, 1)
                pool.wait_ge(mirrored, 3 * k + 3)
                pool.dma_start(inv_d[which][2 * CPB * b:2 * CPB * (b + 1)].rearrange("c h i j -> (c h) (i j)"),
                               upper[:].rearrange("p i j -> p (i j)")).then_inc(inv_stored[k], 16)

            pool.wait_ge(sgn_copied, 8)
            def norm3(i, par):
                c = 2 * i + par
                wait(pool, ve3_ready, c + 1)
                nc.gpsimd.tensor_tensor(rs3[:], ve3[:], half_neg[:, 0:1], ALU.pow).then_inc(rs3_ready, 1)

            def small_load(b):
                for n in range(2):
                    pool.wait_ge(factors_stored[n], 64 * PAIRS_B * (b + 1))
                if b:
                    pool.wait_ge(minv_stored[b - 1], 16)
                pool.dma_start(msw[:, 0], m_d[2 * CPB * b:2 * CPB * (b + 1)].rearrange("c h i j -> (c h) i j")
                               ).then_inc(m_loaded, 16)

            def small_finish(b):
                pool.wait_ge(m_inverted, b + 1)
                pool.dma_start(minv_d[2 * CPB * b:2 * CPB * (b + 1)].rearrange("c h i j -> (c h) (i j)"),
                               msw[:, 0].rearrange("p i j -> p (i j)")).then_inc(minv_stored[b], 16)

            def norms(b):
                each_pair(pool, PAIRS_B * b, PAIRS_B * (b + 1), norm3)

            load(0)
            for k in range(3):
                load(k + 1)
                finish(k)
            load(4)
            finish(3)
            small_load(0)
            load(5)
            finish(4)
            small_finish(0)
            load(6)
            norms(0)
            finish(5)
            small_load(1)
            load(7)
            finish(6)
            small_finish(1)
            norms(1)
            finish(7)
            for b in (2, 3):
                small_load(b)
                small_finish(b)
                norms(b)

        @block.scalar
        def _(act):
            act.wait_ge(ffw_loaded, 32)
            for t in range(FT):
                if t:
                    act.wait_ge(abs_done, t)
                nc.scalar.activation(absw[:, 0:DM], w1n[:, t], ACT.Abs, accum_out=alpha1[:, t:t + 1]).then_inc(abs_done, 1)
            for t in range(KT):
                act.wait_ge(abs_done, FT + t)
                nc.scalar.activation(absw, w2n[:, t], ACT.Abs, accum_out=alpha2[:, t:t + 1]).then_inc(abs_done, 1)
            act.wait_ge(abs_done, FT + KT)
            nc.scalar.activation(w1n, w1n, ACT.Sign).then_inc(sign_done, 1)
            nc.scalar.activation(w2n, w2n, ACT.Sign).then_inc(sign_done, 1)
            nc.scalar.mul(alpha1[:], alpha1[:], 1.0 / DM).then_inc(alpha_done, 1)
            nc.scalar.mul(alpha2[:], alpha2[:], 1.0 / FF).then_inc(alpha_done, 1)
            act.wait_ge(alpha_done, 2)
            act.wait_ge(zeroed, 2)
            for t in range(KT):
                nc.scalar.activation(diag[:, t], ident[:], ACT.Copy, scale=alpha2[:, t:t + 1]).then_inc(diag_done, 1)
            for n in range(8):
                act.wait_ge(sgn_ready, n + 1)
                if n < 4:
                    dst = s1t[:, n // 2, (n % 2) * BANK:(n % 2 + 1) * BANK]
                else:
                    dst = s2t[:, 2 * (n - 4):2 * (n - 3)].rearrange("p t d -> p (t d)")
                nc.scalar.copy(dst, bank[n][:]).then_inc(sgn_copied, 1)
            act.wait_ge(alpha_bcast, 1)
            nc.scalar.copy(alpha2r[:], bank[0][:, 0:DM]).then_inc(alpha_row, 1)

            act.wait_ge(consts_loaded, 48)

            def copy_gc(i, par):
                c = 2 * i + par
                wait(act, gc_stored[par], 32 * i)
                for j in range(2):
                    wait(act, gc_ready, 2 * c + j + 1)
                    nc.scalar.copy(gc[:, par, 4 * j:4 * j + 4].rearrange("p h n -> p (h n)"), bank[4 + j][:]
                                   ).then_inc(gc_copied, 1)

            def project(i, par, lead):
                c = 2 * i + par
                wait(act, xnt_ready, c + 1)
                for t in range(KT):
                    ins = nc.scalar.activation(xnt[:, par, t], bank[0][:, P * t:P * (t + 1)], ACT.Identity,
                                               scale=gain[:, t:t + 1], bias=bias[:, t:t + 1])
                ins.then_inc(xnt_copied, 1)
                if not lead or par == 1:
                    copy_gc(i if par else i - 1, 1 - par)
                for n in range(6):
                    if n == 4:
                        wait(act, q_stored[par], 16 * i)
                    wait(act, kvq_ready, 6 * c + n + 1)
                    if n < 4:
                        dst = kv[:, par, n // 2, (n % 2) * BANK:(n % 2 + 1) * BANK]
                    else:
                        dst = qt[:, par, 4 * (n - 4):4 * (n - 3)].rearrange("p h r -> p (h r)")
                    nc.scalar.copy(dst, bank[1 + n % 3][:]).then_inc(kvq_copied, 1)

            def schur(i, par):
                c = 2 * i + par
                wait(act, t_ready, c + 1)
                nc.scalar.copy(xs[:].rearrange("p h j -> p (h j)"), bank[6][:, 0:PAIRS * HALF]).then_inc(t_copied, 1)
                wait(act, schur_ready, c + 1)
                wait(act, schur_stored[par], 32 * i)
                nc.scalar.copy(sch[:, par].rearrange("p h j -> p (h j)"), bank[7][:, 0:PAIRS * HALF]).then_inc(schur_copied, 1)

            def chunk(a, b):
                def flat(t):
                    return t.rearrange("p h n -> p (h n)")
                if a:
                    i, par = a
                    c = 2 * i + par
                    wait(act, y_ready, c + 1)
                    nc.scalar.copy(flat(ysb[:]), bank[0][:]).then_inc(y_copied, 1)
                if b:
                    j, q = b
                    d = 2 * j + q
                    wait(act, nz_ready, d + 1)
                    nc.scalar.mul(flat(nz[:]), bank[5][0:2 * RANK, :], -1.0).then_inc(nz_copied, 1)
                if a:
                    wait(act, w2_ready, c + 1)
                    nc.scalar.copy(flat(w2sb[:]), bank[2][:]).then_inc(w2_copied, 1)
                if b:
                    for n in range(2):
                        wait(act, ot_ready, 2 * d + n + 1)
                        nc.scalar.mul(ot[:, 4 * n:4 * n + 4].rearrange("p h r -> p (h r)"), bank[6 + n][:], SCALE
                                      ).then_inc(ot_copied, 1)
                if a:
                    wait(act, w_ready, c + 1)
                    wait(act, wbd_copied, 2 * c)
                    nc.scalar.mul(flat(wt[:]), bank[2][:], -1.0).then_inc(w_copied, 1)
                if b:
                    wait(act, y3t_ready, d + 1)
                    nc.scalar.copy(y3t[:].rearrange("p t r -> p (t r)"), bank[5][:, 0:DM]).then_inc(y3t_copied, 1)
                    for t in range(FT):
                        if t % 4 == 0:
                            wait(act, h_ready, FT * d + t + 4)
                        nc.scalar.activation(ht[:, t], bank[6 + t // 4][:, P * (t % 4):P * (t % 4 + 1)], ACT.Gelu,
                                             scale=alpha1[:, t:t + 1], bias=b1c[:, t:t + 1]).then_inc(h_copied, 1)
                if a:
                    wait(act, factors_stored[par], 64 * i)
                    wait(act, z_ready, c + 1)
                    nc.scalar.copy(zs[:, par], bank[0][0:2 * RANK, :]).then_inc(z_copied, 1)
                    for n in range(2):
                        wait(act, yt_ready, 2 * c + n + 1)
                        nc.scalar.copy(yts[:, par, BANK * n:BANK * (n + 1)], bank[3 + n][0:2 * RANK, :]).then_inc(yt_copied, 1)

            def project_all(b):
                first, last = PAIRS_B * b, PAIRS_B * (b + 1)
                for par in range(2):
                    project(first, par, True)
                with act.Fori(first + 1, last) as i:
                    for par in range(2):
                        project(i, par, False)
                copy_gc(last - 1, 1)

            for stage, *at in PROGRAM:
                if stage == "project":
                    project_all(*at)
                elif stage == "schur":
                    each_pair(act, PAIRS_B * at[0], PAIRS_B * (at[0] + 1), schur)
                elif stage == "fused":
                    fused_pairs(act, at[0], at[1], chunk)

        @block.vector
        def _(dve):
            V = nc.vector
            dve.wait_ge(zeroed, 4)
            step = [0]

            def link(ins):
                step[0] += 1
                ins.then_inc(ln_step, 1)

            def settle():
                dve.wait_ge(ln_step, step[0])

            def statistics(src, moments, var_eps):
                for k in range(GROUP):
                    link(V.bn_stats(stats[:, k], src[:, k]))
                settle()
                for k in range(GROUP):
                    link(V.bn_aggr(moments[:, k], stats[:, k]))
                settle()
                V.tensor_scalar(var_eps, moments[:, :, 1], LN_EPS, None, ALU.add).then_inc(veps_ready, 1)

            for g in range(NCH // GROUP):
                n = g % 2
                dve.wait_ge(x_loaded[n], 16 * (g // 2 + 1))
                statistics(xg[:, n], mv, veps[:])
                if g >= 2:
                    dve.wait_ge(ln_stored[(g - 2) * GROUP // CPB], 64 if (g - 2) % 2 else 32)
                dve.wait_ge(rstd_ready, 2 * g + 1)
                for k in range(GROUP):
                    link(V.tensor_scalar(lng[:, n, k], xg[:, n, k], mv[:, k, 0:1], rstd[:, k:k + 1],
                                         ALU.subtract, ALU.mult))
                settle()
                statistics(lng[:, n], mv2, veps2[:])
                dve.wait_ge(rstd_ready, 2 * g + 2)
                for k in range(GROUP):
                    link(V.tensor_scalar(hatg[:, n, k], lng[:, n, k], mv2[:, k, 0:1], rstd2[:, k:k + 1],
                                         ALU.subtract, ALU.mult))
                settle()
                V.tensor_tensor(lng[:, n], lng[:, n], xg[:, n], ALU.add).then_inc(hat_ready, 1)

            done = [0]

            def pivot(src, dst, size, strips, count, wait_first):
                n = size
                if wait_first is not None:
                    dve.wait_ge(swept, wait_first)
                V.reciprocal(piv[:], src[:, 0, 0:1]).then_inc(swept, 1)
                dve.wait_ge(swept, count + 1)
                V.tensor_scalar(prow[:, 1:n], src[:, 0, 1:n], piv[:], None, ALU.mult).then_inc(swept, 1)
                V.tensor_scalar(dst[:, 0:n - 1, n - 1], src[:, 0, 1:n], piv[:], None, ALU.mult).then_inc(swept, 1)
                V.tensor_scalar(dst[:, n - 1, n - 1:n], piv[:], -1.0, None, ALU.mult).then_inc(swept, 1)
                dve.wait_ge(swept, count + 2)
                at = 0
                tiles = []
                for r0, r1 in strips:
                    rows, cols = r1 - r0, n - 1 - r0
                    t = outer[:, at:at + rows * cols].rearrange("p (i j) -> p i j", i=rows)
                    at += rows * cols
                    tiles.append(t)
                    V.tensor_tensor(t, src[:, 0, r0 + 1:r1 + 1].unsqueeze(2).broadcast_to([P, rows, cols]),
                                    prow[:, r0 + 1:n].unsqueeze(1).broadcast_to([P, rows, cols]), ALU.mult).then_inc(swept, 1)
                for m, (r0, r1) in enumerate(strips):
                    dve.wait_ge(swept, count + 4 + m + 1)
                    V.tensor_tensor(dst[:, r0:r1, r0:n - 1], src[:, r0 + 1:r1 + 1, r0 + 1:n], tiles[m],
                                    ALU.subtract).then_inc(swept, 1)

            STRIPS = [(0, 16), (16, 31)]
            PER = 4 + 2 * len(STRIPS)

            def square(k, n):
                return work[:, 2 * (k % 2) + n, :].rearrange("p (i j) -> p i j", i=HALF)

            def begin(k):
                dve.wait_ge(sweep_loaded[k % 2], 16 * (k // 2 + 1))
                dg = work[:, 2 * (k % 2), 0:HALF * HALF:HALF + 1]
                V.tensor_scalar(dg, dg, RIDGE, None, ALU.add).then_inc(swept, 1)
                if k < 2:
                    V.memset(square(k, 1)[:], 0.0).then_inc(swept, 1)
                    done[0] += 1
                done[0] += 1

            def two_pivots(k, count):
                pivot(square(k, 0), square(k, 1), HALF, STRIPS, count, count)
                pivot(square(k, 1), square(k, 0), HALF, STRIPS, count + PER, count + PER)

            def end(k, base):
                done[0] = base + HALF * PER
                dve.wait_ge(swept, done[0])
                V.tensor_copy(piv[:], piv[:]).then_inc(inverted, 1)

            def sweep(k):
                begin(k)
                base = done[0]
                with dve.Fori(0, HALF // 2) as t:
                    two_pivots(k, t * (2 * PER) + base)
                end(k, base)

            def small_sweep(b):
                a, z = msw[:, 0], msw[:, 1]
                strips = [(0, RANK - 1)]
                per = 4 + 2 * len(strips)
                dve.wait_ge(m_loaded, 16 * (b + 1))
                V.memset(z[:], 0.0).then_inc(swept, 1)
                done[0] += 1
                count = done[0]
                for t in range(RANK):
                    src, dst = (a, z) if t % 2 == 0 else (z, a)
                    pivot(src, dst, RANK, strips, count, count)
                    count += per
                done[0] = count
                dve.wait_ge(swept, count)
                for r in range(1, RANK):
                    V.tensor_copy(a[:, r, 0:r], a[:, 0:r, r]).then_inc(swept, 1)
                done[0] += RANK - 1
                dve.wait_ge(swept, done[0])
                V.tensor_copy(piv[:], piv[:]).then_inc(m_inverted, 1)

            def chunk(a, b, pivots):
                def flat(t):
                    return t.rearrange("p h n -> p (h n)")
                def banked(n, width):
                    return bank[n][:].rearrange("p (h n) -> p h n", n=width)
                if a:
                    i, par = a
                    c = 2 * i + par
                    wait(dve, g1_ready, c + 1)
                    V.tensor_tensor(rsb[:], banked(1, HD), gct[:, par, :, HD:2 * HD], ALU.add).then_inc(r1_done, 1)
                if b:
                    j, q = b
                    d = 2 * j + q
                    wait(dve, wr_ready, d + 1)
                    for s in range(2):
                        sl = slice(HD * s, HD * (s + 1))
                        V.scalar_tensor_tensor(out=state[sl, q, :, sl], in0=state[sl, 1 - q, :, sl], scalar=DECAY,
                                               in1=banked(5, HD)[sl], op0=ALU.mult, op1=ALU.add).then_inc(state_done, 1)
                if a:
                    wait(dve, g2_ready, c + 1)
                    V.tensor_tensor(r2sb[:], banked(1, HD), gct[:, par, :, HD:2 * HD], ALU.add).then_inc(r2_done, 1)
                if b:
                    wait(dve, wo_ready, d + 1)
                    V.tensor_tensor(x2[:], bank[5][:, 0:DM], resl[:, q], ALU.add).then_inc(x2_done, 1)
                    wait(dve, x2_done, d + 1)
                    V.bn_stats(st3[:], x2[:]).then_inc(ln3_step, 1)
                    wait(dve, ln3_step, 2 * d + 1)
                    V.tensor_tensor(x2b[:], x2[:], b2r[:], ALU.add).then_inc(x2b_done, 1)
                    V.bn_aggr(mv3[:], st3[:]).then_inc(ln3_step, 1)
                    wait(dve, ln3_step, 2 * d + 2)
                    V.tensor_scalar(ve3[:], mv3[:, 1:2], LN_EPS, None, ALU.add).then_inc(ve3_ready, 1)
                pivots(0)
                if a:
                    wait(dve, w_copied, c + 1)
                    wait(dve, wbdt_ready, 2 * c)
                    for s in range(2):
                        sl = slice(HD * s, HD * (s + 1))
                        V.tensor_copy(wbd[sl, :, sl], wt[sl]).then_inc(wbd_copied, 1)
                    for n in range(2):
                        wait(dve, wbdt_ready, 2 * c + n + 1)
                        V.tensor_copy(flat(wbdt[:, 4 * n:4 * n + 4]), bank[3 + n][:]).then_inc(wbdt_copied, 1)
                if b:
                    wait(dve, rs3_ready, d + 1)
                    V.tensor_scalar(x3[:], x2[:], mv3[:, 0:1], rs3[:], ALU.subtract, ALU.mult).then_inc(x3_ready, 1)
                if a:
                    wait(dve, y2_ready, c + 1)
                    wait(dve, yt_ready, 2 * c)
                    y2 = bank[1][:, 0:PAIRS * RANK].rearrange("p (h n) -> p h n", n=RANK)
                    for s in range(2):
                        sl = slice(HD * s, HD * (s + 1))
                        V.tensor_copy(y2bd[sl, :, RANK * s:RANK * (s + 1)], y2[sl]).then_inc(y2_copied, 1)
                    wait(dve, m_ready, c + 1)
                    wait(dve, factors_stored[par], 64 * i)
                    V.tensor_copy(ms[:, par], bank[1][0:2 * RANK, 256:256 + 2 * RANK * PAIRS]).then_inc(m_copied, 1)
                pivots(1)
                if b:
                    wait(dve, o_ready, d + 1)
                    V.tensor_tensor(ysc[:], bank[5][:, 0:DM], alpha2r[:], ALU.mult).then_inc(scaled, 1)
                    wait(dve, scaled, d + 1)
                    wait(dve, x2b_done, d + 1)
                    wait(dve, out_stored[q], 16 * j)
                    V.tensor_tensor(yo[:, q], ysc[:], x2b[:], ALU.add).then_inc(o_done, 1)

            dve.wait_ge(alpha_row, 1)
            dve.wait_ge(zeroed, 11)
            dve.wait_ge(b2_loaded, 16)
            def fused(a, b, k):
                if b:
                    dve.wait_ge(ot_ready, 2 * CPB * b)
                    V.memset(state[:, 1], 0.0).then_inc(state_cleared, 1)
                    dve.wait_ge(state_cleared, b)
                if k is not None:
                    begin(k)
                base = done[0]
                first = PAIRS_B * (b if b is not None else a)
                each = HALF // CPB

                def beside(i_a, i_b):
                    i, par = i_b or i_a
                    count = (base - first * 2 * each * PER + par * each * PER) + i * (2 * each * PER)
                    chunk(i_a, i_b, (lambda n: two_pivots(k, count + 2 * n * PER)) if k is not None else lambda n: None)

                fused_pairs(dve, a, b, beside)
                if k is not None:
                    end(k, base)

            for stage, *at in PROGRAM:
                if stage == "sweep":
                    sweep(*at)
                elif stage == "small":
                    small_sweep(*at)
                elif stage == "fused":
                    fused(*at)

        @block.tensor
        def _(pe):
            mm = nc.tensor.matmul
            pe.wait_ge(zeroed, 2)
            pe.wait_ge(sign_done, 2)
            for n in range(8):
                for t in range(4):
                    if n < 4:
                        src = w1n[:, 4 * (n % 2) + t, P * (n // 2):P * (n // 2 + 1)]
                    else:
                        src = w2n[:, t % 2, P * (2 * (n - 4) + t // 2):P * (2 * (n - 4) + t // 2 + 1)]
                    ins = nc.tensor.transpose(bank[n][:, P * t:P * (t + 1)], src, ident[:])
                ins.then_inc(sgn_ready, 1)
            pe.wait_ge(diag_done, 2)
            pe.wait_ge(zeroed, 4)
            pe.wait_ge(sgn_copied, 8)
            mm(bank[0][:, 0:DM], ones[:], diag[:].rearrange("p t d -> p (t d)"), start=True, stop=True).then_inc(alpha_bcast, 1)
            pe.wait_ge(alpha_row, 1)
            pe.wait_ge(qkv_loaded, 64)

            def gram(i, par):
                c = 2 * i + par
                wait(pe, kvq_copied, 6 * c + 4)
                for j in range(2):
                    wait(pe, gc_copied, 2 * c + j - 1)
                    for h in range(8 * j, 8 * j + 8):
                        cols = slice(HD * h, HD * (h + 1))
                        lo = HD * (h % 2)
                        at = 2 * HD * (h // 2 % 4)
                        ins = mm(bank[4 + j][lo:lo + HD, at:at + 2 * HD], kv[:, par, 0, cols], kv[:, par, :, cols],
                                 start=True, stop=True)
                    ins.then_inc(gc_ready, 1)

            def project(i, par, lead):
                c = 2 * i + par
                wait(pe, xhat_loaded[par], 16 * (i + 1))
                wait(pe, xnt_copied, c)
                for t in range(KT):
                    ins = nc.tensor.transpose(bank[0][:, P * t:P * (t + 1)], xh[:, par, P * t:P * (t + 1)], ident[:])
                ins.then_inc(xnt_ready, 1)
                if not lead or par == 1:
                    gram(i if par else i - 1, 1 - par)
                wait(pe, xnt_copied, c + 1)
                for n in range(6):
                    wait(pe, kvq_copied, 6 * c + n - 2)
                    dst = bank[1 + n % 3]
                    if n < 4:
                        for t in range(KT):
                            ins = mm(dst[:], xnt[:, par, t], wqkv[:, n // 2, t, (n % 2) * BANK:(n % 2 + 1) * BANK],
                                     start=t == 0, stop=t == KT - 1)
                    else:
                        for h in range(4):
                            cols = slice(P * (4 * (n - 4) + h), P * (4 * (n - 4) + h + 1))
                            for t in range(KT):
                                ins = mm(dst[:, P * h:P * (h + 1)], wqkv[:, 2, t, cols], xnt[:, par, t],
                                         start=t == 0, stop=t == KT - 1)
                    ins.then_inc(kvq_ready, 1)

            def schur(i, par):
                c = 2 * i + par
                wait(pe, blocks_loaded[par], 96 * (i + 1))
                wait(pe, t_copied, c)
                for h in range(PAIRS):
                    ins = mm(bank[6][:, HALF * h:HALF * (h + 1)], pbd[:, par, h], gct[:, par, h, HALF:HD], start=True, stop=True)
                ins.then_inc(t_ready, 1)
                wait(pe, schur_copied, c)
                mm(bank[7][:, 0:HALF * PAIRS], ident[:], gct[:, par, :, HALF:HD], start=True, stop=False,
                   skip_group_check=True)
                wait(pe, t_copied, c + 1)
                for h in range(PAIRS):
                    ins = mm(bank[7][:, HALF * h:HALF * (h + 1)], gbd[:, par, h], xs[:, h], start=False, stop=h == PAIRS - 1,
                             skip_group_check=True)
                ins.then_inc(schur_ready, 1)

            def chunk(a, b):
                def at(n, h, w=HD):
                    return bank[n][:, w * h:w * (h + 1)]
                if a:
                    i, par = a
                    c = 2 * i + par
                    wait(pe, solve_loaded[par], 128 * (i + 1))
                    wait(pe, z_copied, c)
                    for h in range(PAIRS):
                        ins = mm(at(0, h), pbd[:, par, h], gct[:, par, h, HD:2 * HD], start=True, stop=True)
                    ins.then_inc(y_ready, 1)
                if b:
                    j, q = b
                    d = 2 * j + q
                    wait(pe, apply_loaded[q], 96 * (j + 1))
                    wait(pe, scaled, d)
                    for h in range(PAIRS):
                        m = mbd[:, q].rearrange("p h n -> p (h n)") if h == 0 else mbd[:, q, h]
                        ins = mm(bank[5][0:m.shape[1], HD * h:HD * (h + 1)], m, zl[:, q, h], start=True, stop=True)
                    ins.then_inc(nz_ready, 1)
                if a:
                    wait(pe, y_copied, c + 1)
                    wait(pe, m_copied, c)
                    for h in range(PAIRS):
                        ins = mm(at(1, h), gbd[:, par, h], ysb[:, h], start=True, stop=True)
                    ins.then_inc(g1_ready, 1)
                if b:
                    wait(pe, nz_copied, d + 1)
                    for h in range(PAIRS):
                        ins = mm(at(5, h), ytl[:, q, h], nz[:, h], start=True, stop=True)
                    ins.then_inc(wr_ready, 1)
                if a:
                    wait(pe, r1_done, c + 1)
                    wait(pe, w_copied, c)
                    for h in range(PAIRS):
                        ins = mm(at(2, h), sbd[:, par, h], rsb[:, h], start=h == 0, stop=False, skip_group_check=True)
                    ins.then_inc(w2_ready, 1)
                if b:
                    wait(pe, state_done, 2 * (d + 1))
                    for n in range(2):
                        wait(pe, h_copied, FT * d - 4 * (1 - n))
                        for h in range(4 * n, 4 * n + 4):
                            ins = mm(bank[6 + n][:, P * (h % 4):P * (h % 4 + 1)], state[:, q, h], qt[:, q, h],
                                     start=True, stop=True)
                        ins.then_inc(ot_ready, 1)
                if a:
                    wait(pe, w2_copied, c + 1)
                    for h in range(PAIRS):
                        ins = mm(at(1, h), gbd[:, par, h], w2sb[:, h], start=True, stop=True)
                    ins.then_inc(g2_ready, 1)
                if b:
                    for h in range(PAIRS):
                        wait(pe, ot_copied, 2 * d + h // 4 + 1)
                        ins = mm(bank[5][:, 0:DM], ot[:, h], wo[:, h], start=h == 0, stop=h == PAIRS - 1)
                    ins.then_inc(wo_ready, 1)
                if a:
                    wait(pe, r2_done, c + 1)
                    for h in range(PAIRS):
                        ins = mm(at(2, h), pbd[:, par, h], r2sb[:, h], start=False, stop=h == PAIRS - 1, skip_group_check=True)
                    ins.then_inc(w_ready, 1)
                    wait(pe, wbd_copied, 2 * (c + 1))
                    wait(pe, yt_copied, 2 * c)
                    for n in range(2):
                        for h in range(4):
                            ins = nc.tensor.transpose(at(3 + n, h, P), wbd[:, 4 * n + h], ident[:])
                        ins.then_inc(wbdt_ready, 1)
                if b:
                    wait(pe, x3_ready, d + 1)
                    for t in range(KT):
                        ins = nc.tensor.transpose(bank[5][:, P * t:P * (t + 1)], x3[:, P * t:P * (t + 1)], ident[:])
                    ins.then_inc(y3t_ready, 1)
                if a:
                    for h in range(PAIRS):
                        wait(pe, wbdt_copied, 2 * c + h // 4 + 1)
                        ins = mm(at(1, h, RANK), wbdt[:, h], wt[:, h, 0:RANK], start=True, stop=True)
                    ins.then_inc(y2_ready, 1)
                if b:
                    wait(pe, y3t_copied, d + 1)
                    for t in range(FT):
                        for k in range(KT):
                            ins = mm(bank[6 + t // 4][:, P * (t % 4):P * (t % 4 + 1)], s1t[:, k, P * t:P * (t + 1)], y3t[:, k],
                                     start=k == 0, stop=k == KT - 1)
                        ins.then_inc(h_ready, 1)
                if a:
                    wait(pe, y2_copied, 2 * (c + 1))
                    for h in range(PAIRS):
                        ins = mm(bank[0][0:2 * RANK, HD * h:HD * (h + 1)], y2bd[:, h], wt[:, h], start=True, stop=True)
                    ins.then_inc(z_ready, 1)
                    for h in range(PAIRS):
                        o = 256 + 2 * RANK * h
                        ins = mm(bank[1][0:2 * RANK, o:o + 2 * RANK], y2bd[:, h], y2bd[:, h], start=True, stop=True)
                    ins.then_inc(m_ready, 1)
                    for n in range(2):
                        for h in range(4):
                            ins = nc.tensor.transpose(bank[3 + n][0:2 * RANK, P * h:P * (h + 1)], y2bd[:, 4 * n + h], ident[:])
                        ins.then_inc(yt_ready, 1)
                if b:
                    for t in range(FT):
                        wait(pe, h_copied, FT * d + t + 1)
                        ins = mm(bank[5][:, 0:DM], ht[:, t], s2t[:, t], start=t == 0, stop=t == FT - 1)
                    ins.then_inc(o_ready, 1)

            def project_all(b):
                first, last = PAIRS_B * b, PAIRS_B * (b + 1)
                for par in range(2):
                    project(first, par, True)
                with pe.Fori(first + 1, last) as i:
                    for par in range(2):
                        project(i, par, False)
                gram(last - 1, 1)

            projected = formed = applied = 0
            for stage, *at in PROGRAM:
                if stage == "project":
                    project_all(*at)
                    projected += CPB
                elif stage == "schur":
                    wait(pe, h_copied, FT * applied)
                    each_pair(pe, PAIRS_B * at[0], PAIRS_B * (at[0] + 1), schur)
                    formed += CPB
                elif stage == "fused":
                    pe.wait_ge(gc_copied, 2 * projected)
                    pe.wait_ge(kvq_copied, 6 * projected)
                    pe.wait_ge(t_copied, formed)
                    pe.wait_ge(schur_copied, formed)
                    fused_pairs(pe, at[0], at[1], chunk)
                    applied += CPB if at[1] is not None else 0


_INS = ["L0_attn_x", "L0_attn_ln_g", "L0_attn_ln_b", "L0_attn_Wq", "L0_attn_Wk", "L0_attn_Wv", "L0_attn_Wo",
        "L0_ffn_w1", "L0_ffn_b1", "L0_ffn_w2", "L0_ffn_b2"]


def kernel(**inputs):
    import numpy as _np
    import concourse.bacc as _bacc
    from concourse import mybir as _mybir
    from concourse.bass_utils import run_bass_kernel_spmd as _run

    nc = _bacc.Bacc("TRN2", target_bir_lowering=False, num_devices=1)
    arrays, args = {}, []
    for name in _INS:
        a = _np.ascontiguousarray(inputs[name])
        arrays[f"in_{name}_dram"] = a
        args.append(nc.dram_tensor(f"in_{name}_dram", a.shape, _mybir.dt.from_np(a.dtype), kind="ExternalInput").ap())
    args.append(nc.dram_tensor("out_0_dram", (BATCH, SEQ, DM), _mybir.dt.float32, kind="ExternalOutput").ap())
    build(nc, *args)
    r = _run(nc, [arrays], core_ids=[0])
    return r.results[0]["out_0_dram"]
```

```python
from contextlib import ExitStack

import concourse.bass as bass
from concourse import mybir

P = 128
ALU = mybir.AluOpType
ACT = mybir.ActivationFunctionType
F32 = mybir.dt.float32
F16 = mybir.dt.float16

BATCH, SEQ, DM = 4, 1024, 256
HEADS, HD, RANK = 16, 64, 8
CHUNK = P
CPB = SEQ // CHUNK
PAIRS_B = CPB // 2
NCH = BATCH * CPB
PAIRS = HEADS // 2
KT = DM // P
HALF = HD // 2
FF = 1024
FT = FF // P
BANK = 512

RIDGE, LN_EPS, SCALE, DECAY = 1e-4, 1e-5, 0.125, 0.9
GROUP = 4

LAG = PAIRS_B + 1
ALL_PAIRS = NCH // 2
CUTS = (1, LAG, LAG + 1, LAG + 2, ALL_PAIRS)

SWEEPS = [(0, 0), (0, 1), (1, 0), (0, 2), (1, 1), (0, 3), (1, 2), (1, 3)]
PROGRAM = [("project", 0), ("load", 0), ("sweep", 0, HALF), ("project", 1), ("load", 1), ("schur", 0), ("load", 2),
           ("sweep", 1, HALF), ("project", 2), ("load", 3), ("sweep", 2, HALF), ("schur", 1), ("sweep", 3, 8), ("load", 4),
           ("joint", 0, 2, 3, 6), ("joint", 2, 4, 4, 8), ("load", 5), ("schur", 2), ("load", 6), ("sweep", 5, 12),
           ("fused", 4, 5, 5, 4, 0), ("fused", 5, 6, 5, 6, None), ("fused", 6, 7, 6, 8, None), ("schur", 3),
           ("sweep", 6, 16), ("load", 7), ("fused", 7, 8, None, 0, None), ("fused", 8, 9, 7, 4, 1),
           ("fused", 9, 11, 7, 6, None),
           ("fused", 11, 12, None, 0, None), ("fused", 12, 13, None, 0, 2), ("fused", 13, 16, None, 0, None),
           ("fused", 16, 17, None, 0, 3), ("fused", 17, 21, None, 0, None)]
PRODUCT_STEPS = (1, 2, 4, 5, 7, 8)
BESIDE = ALL_PAIRS - PAIRS_B
NZ_BANK, WR_BANK, OT_BANKS = (6, 0), (6, 1), ((7, 6), (3, 4))
SLOTS = {0: (0, 0, 0, 0), 4: (1, 1, 2, 0), 6: (1, 1, 3, 1), 8: (1, 2, 3, 2)}


def merged(program):
    stages = []
    for stage, *at in program:
        if stage in ("load", "sweep"):
            continue
        if stage in ("joint", "fused"):
            if stages and stages[-1][0] == stage:
                stages[-1] = (stage, stages[-1][1], at[1])
            else:
                stages.append((stage, at[0], at[1]))
        else:
            stages.append((stage, *at))
    return stages


def build(nc, x, ln_g, ln_b, Wq, Wk, Wv, Wo, w1, b1, w2, b2, out):
    x_rows = x.rearrange("b s d -> (b s) d")
    x_groups = x_rows.rearrange("(g k p) d -> g p k d", p=P, k=GROUP)
    out_chunks = out.rearrange("b s d -> (b s) d").rearrange("(c p) d -> c p d", p=P)

    def scratch(name, shape):
        return nc.dram_tensor(name, shape, F32, kind="Internal").ap()

    xhat_d = scratch("xhat_d", [NCH, P, DM])
    res_d = scratch("res_d", [NCH, P, DM])
    gc_d = scratch("gc_d", [NCH, PAIRS, 2 * HD, 2 * HD])
    q_d = scratch("q_d", [NCH, P, PAIRS, P])
    schur_d = scratch("schur_d", [NCH, P, P])
    inv_d = [scratch(f"inv{k}_d", [NCH, PAIRS, 2, HALF, HALF]) for k in range(2)]
    z_d = scratch("z_d", [NCH, P, 2 * HD])
    yt_d = scratch("yt_d", [NCH, P, 2 * P])
    m_d = scratch("m_d", [2 * NCH, PAIRS, RANK, RANK])
    minv_d = scratch("minv_d", [2 * NCH, PAIRS, RANK, RANK])

    with ExitStack() as ctx:
        def sb(name, shape, dt=F32):
            return ctx.enter_context(nc.sbuf_tensor(name, shape, dt))

        def sem(name):
            return ctx.enter_context(nc.semaphore(name))

        bank = [ctx.enter_context(nc.psum_tensor(f"bank{n}", [P, BANK], F32)) for n in range(8)]

        wqkv = sb("wqkv", [P, 3, KT, HEADS * HD])
        wo = sb("wo", [P, PAIRS, DM])
        s1t = sb("s1t", [P, KT, FF], F16)
        s2t = sb("s2t", [P, FT, DM], F16)
        ident = sb("ident", [P, P])
        ident16 = sb("ident16", [P, P], F16)
        ones = sb("ones", [P, P])
        diag = sb("diag", [P, KT, P])
        gain = sb("gain", [P, KT])
        bias = sb("bias", [P, KT])
        b1c = sb("b1c", [P, FT])
        b2r = sb("b2r", [P, DM])
        alpha1 = sb("alpha1", [P, FT])
        alpha2 = sb("alpha2", [P, KT])
        alpha2r = sb("alpha2r", [P, DM])
        half_neg = sb("half_neg", [P, GROUP])
        work = sb("work", [P, 4, HALF * HALF])
        w1n = work[:, 0:2, :].rearrange("p a n -> p (a n)").rearrange("p (t d) -> p t d", d=DM)
        w2n = work[:, 2:4, :]
        early = sb("early", [P, 3 * 2 * GROUP * DM])
        xg, lng, hatg = (early[:, 2 * GROUP * DM * n:2 * GROUP * DM * (n + 1)].rearrange(
            "p (a k d) -> p a k d", a=2, k=GROUP) for n in range(3))
        stats = sb("stats", [P, GROUP, 6])
        mv = sb("mv", [P, GROUP, 2])
        mv2 = sb("mv2", [P, GROUP, 2])
        veps = sb("veps", [P, GROUP])
        veps2 = sb("veps2", [P, GROUP])
        rstd = sb("rstd", [P, GROUP])
        rstd2 = sb("rstd2", [P, GROUP])
        xh = sb("xh", [P, 2, DM])
        xnt = sb("xnt", [P, 2, KT, P])
        kv = sb("kv", [P, 2, 2, HEADS * HD])
        absw = kv[:, 0, 0, :]
        qt = sb("qt", [P, 2, PAIRS, P])
        gc = sb("gc", [P, 2, PAIRS, 2 * HD])
        gct = sb("gct", [P, 2, PAIRS, 2 * HD])
        gbd = sb("gbd", [P, 2, PAIRS, P])
        pbd = sb("pbd", [P, 2, PAIRS, P])
        sbd = sb("sbd", [P, 2, PAIRS, P])
        xs = sb("xs", [P, 2, 2, PAIRS // 2, HD])
        sch = sb("sch", [P, 2, 2 * HD])
        upper = sb("upper", [P, HALF, HALF])
        lower = sb("lower", [P, HALF, HALF])
        piv = sb("piv", [P, 1])
        prow = sb("prow", [P, HALF])
        outer = sb("outer", [P, 16 * 31 + 15 * 15])
        used = [0]

        def late(*dims):
            size = 1
            for n in dims:
                size *= n
            part = early[:, used[0]:used[0] + size]
            used[0] += size
            assert used[0] <= early.shape[1]
            return part.rearrange("p (a b) -> p a b", a=dims[0]) if len(dims) == 2 else part

        ysb, rsb, w2sb, r2sb, wt = (late(PAIRS, HD) for _ in range(5))
        tts = ysb.rearrange("p (a h) n -> p a (h n)", a=2)
        wbd = sb("wbd", [P, PAIRS, P])
        wbdt = late(PAIRS, P)
        we = sb("we", [P, PAIRS, 2 * RANK])
        y2bd = late(PAIRS // 4, P)
        zs = sb("zs", [P, 2, 2 * HD])
        yts = sb("yts", [P, 2, 2 * P])
        ms = sb("ms", [2 * RANK, 2, PAIRS * 2 * RANK])
        msw = sb("msw", [P, 2, RANK, RANK])
        zl = sb("zl", [2 * RANK, 2, PAIRS, HD])
        ytl = sb("ytl", [2 * RANK, 2, PAIRS, P])
        mbd = sb("mbd", [2 * RANK, 2, PAIRS, 2 * RANK])
        nz = sb("nz", [2 * RANK, PAIRS, HD])
        state = sb("state", [P, 2, PAIRS, P])
        ot = kv[:, 0, 0, :].rearrange("p (h r) -> p h r", h=PAIRS)
        ht = kv[:, 0, 1, :].rearrange("p (t r) -> p t r", t=FT)
        resl = late(2, DM)
        hsplit = sb("hsplit", [P, 2, FT, P], F16)
        x3split = sb("x3split", [P, 2, DM], F16)
        x2, x2b, x3, ysc = (late(DM) for _ in range(4))
        st3 = sb("st3", [P, 6])
        mv3 = sb("mv3", [P, 2])
        ve3 = sb("ve3", [P, 1])
        rs3 = sb("rs3", [P, 1])
        unused = sb("unused", [P, 1])
        y3t = sb("y3t", [P, 2, KT, P], F16)
        yo = late(2, DM)

        consts_loaded = sem("consts_loaded")
        qkv_loaded = sem("qkv_loaded")
        ffw_loaded = sem("ffw_loaded")
        b2_loaded = sem("b2_loaded")
        zeroed = sem("zeroed")
        abs_done = sem("abs_done")
        alpha_done = sem("alpha_done")
        sign_done = sem("sign_done")
        diag_done = sem("diag_done")
        sgn_ready = sem("sgn_ready")
        sgn_copied = sem("sgn_copied")
        alpha_bcast = sem("alpha_bcast")
        alpha_row = sem("alpha_row")
        x_loaded = [sem(f"x_loaded{n}") for n in range(2)]
        ln_step = sem("ln_step")
        veps_ready = sem("veps_ready")
        rstd_ready = sem("rstd_ready")
        hat_ready = sem("hat_ready")
        ln_stored = [sem(f"ln_stored{g}") for g in range(NCH // GROUP)]
        xhat_loaded = [sem(f"xhat_loaded{n}") for n in range(2)]
        xnt_ready = sem("xnt_ready")
        xnt_copied = sem("xnt_copied")
        kvq_ready = sem("kvq_ready")
        kvq_copied = sem("kvq_copied")
        gc_ready = sem("gc_ready")
        gc_copied = sem("gc_copied")
        gc_stored = [sem(f"gc_stored{n}") for n in range(2)]
        q_stored = [sem(f"q_stored{n}") for n in range(2)]
        blocks_loaded = [sem(f"blocks_loaded{n}") for n in range(2)]
        t_ready = sem("t_ready")
        t_copied = sem("t_copied")
        eye_placed = sem("eye_placed")
        turned_ready, turned_copied = sem("turned_ready"), sem("turned_copied")
        schur_ready = sem("schur_ready")
        schur_copied = sem("schur_copied")
        schur_stored = [sem(f"schur_stored{n}") for n in range(2)]
        sweep_loaded = [sem(f"sweep_loaded{n}") for n in range(2)]
        swept = sem("swept")
        inverted = sem("inverted")
        mirrored = sem("mirrored")
        inv_stored = [sem(f"inv_stored{k}") for k in range(len(SWEEPS))]
        solve_loaded = [sem(f"solve_loaded{n}") for n in range(2)]
        y_ready, y_copied = sem("y_ready"), sem("y_copied")
        g1_ready, r1_done = sem("g1_ready"), sem("r1_done")
        w2_ready, w2_copied = sem("w2_ready"), sem("w2_copied")
        g2_ready, r2_done = sem("g2_ready"), sem("r2_done")
        w_ready, w_copied = sem("w_ready"), sem("w_copied")
        wbd_copied = sem("wbd_copied")
        wbdt_ready, wbdt_copied = sem("wbdt_ready"), sem("wbdt_copied")
        y2_ready, y2_copied = sem("y2_ready"), sem("y2_copied")
        z_ready, z_copied = sem("z_ready"), sem("z_copied")
        m_ready, m_copied = sem("m_ready"), sem("m_copied")
        yt_ready, yt_copied = sem("yt_ready"), sem("yt_copied")
        factors_stored = [sem(f"factors_stored{n}") for n in range(2)]
        m_loaded = sem("m_loaded")
        m_inverted = sem("m_inverted")
        minv_stored = [sem(f"minv_stored{n}") for n in range(BATCH)]
        apply_loaded = [sem(f"apply_loaded{n}") for n in range(2)]
        nz_ready, nz_copied = sem("nz_ready"), sem("nz_copied")
        wr_ready = sem("wr_ready")
        state_cleared = sem("state_cleared")
        state_done = sem("state_done")
        ot_ready, ot_copied = sem("ot_ready"), sem("ot_copied")
        wo_ready = sem("wo_ready")
        x2_done = sem("x2_done")
        x2b_done = sem("x2b_done")
        ln3_step = sem("ln3_step")
        ve3_ready, rs3_ready, x3_ready = sem("ve3_ready"), sem("rs3_ready"), sem("x3_ready")
        y3t_ready, y3t_copied = sem("y3t_ready"), sem("y3t_copied")
        h_ready, h_copied = sem("h_ready"), sem("h_copied")
        high_done, low_done = sem("high_done"), sem("low_done")
        ident16_done = sem("ident16_done")
        o_ready, scaled, o_done = sem("o_ready"), sem("scaled"), sem("o_done")
        out_stored = [sem(f"out_stored{n}") for n in range(2)]

        block = ctx.enter_context(nc.Block())

        def wait(eng, s, value):
            if isinstance(value, int) and value <= 0:
                return
            eng.wait_ge(s, value)

        def each_two_pairs(eng, b, body):
            first = PAIRS_B // 2 * b
            if first == 0:
                for v in range(2):
                    body(v, v)
                first = 1
            with eng.Fori(first, PAIRS_B // 2 * (b + 1)) as g:
                for v in range(2):
                    body(2 * g + v, v)

        def schur_columns(v):
            return slice(HALF * (1 + v), HALF * (2 + v))

        def fused_pairs(eng, lo, hi, chunk):
            while lo < hi:
                stop = min([cut for cut in CUTS if cut > lo] + [hi])
                stop = min(stop, hi)
                has_a, has_b, has_e = lo < ALL_PAIRS, lo >= LAG, lo > LAG

                def pair(i):
                    for par in range(2):
                        chunk((i, par) if has_a else None, (i - LAG, par) if has_b else None,
                              ((i - LAG, 0) if has_b and par else (i - LAG - 1, 1) if has_e else None))

                if stop - lo == 1:
                    pair(lo)
                else:
                    with eng.Fori(lo, stop) as i:
                        pair(i)
                lo = stop

        LAST = (ALL_PAIRS - 1, 1)

        @block.sync
        def _(sp):
            sp.dma_start(gain[:], ln_g.rearrange("(t p) -> p t", p=P), allow_slow_non_contiguous=True).then_inc(consts_loaded, 16)
            sp.dma_start(bias[:], ln_b.rearrange("(t p) -> p t", p=P), allow_slow_non_contiguous=True).then_inc(consts_loaded, 16)
            sp.dma_start(b1c[:], b1.rearrange("(t p) -> p t", p=P), allow_slow_non_contiguous=True).then_inc(consts_loaded, 16)
            sp.dma_start(w1n, w1.rearrange("(t p) d -> p t d", p=P)).then_inc(ffw_loaded, 16)
            sp.dma_start(w2n, w2.rearrange("(t p) h -> p t h", p=P)).then_inc(ffw_loaded, 16)
            for n, w in enumerate((Wk, Wv, Wq)):
                sp.dma_start(wqkv[:, n], w.rearrange("(t p) h -> p t h", p=P)).then_inc(qkv_loaded, 16)
            sp.dma_start(wo[:], Wo.rearrange("(h p) d -> p h d", p=P)).then_inc(qkv_loaded, 16)
            sp.dma_start(b2r[:], b2.rearrange("(a d) -> a d", a=1).broadcast_to([P, DM])).then_inc(b2_loaded, 16)

            def store_gc(i, par):
                wait(sp, gc_copied, 2 * (2 * i + par + 1))
                sp.dma_start(gc_d[bass.ds(2 * i + par, 1)].rearrange("c h r n -> (c r) h n"), gc[:, par]
                             ).then_inc(gc_stored[par], 16)

            def store_q(i, par):
                wait(sp, kvq_copied, 6 * (2 * i + par + 1))
                sp.dma_start(q_d[bass.ds(2 * i + par, 1)].rearrange("a p h r -> (a p) h r"),
                             qt[:, par]).then_inc(q_stored[par], 16)

            def project(i, par, lead):
                c = 2 * i + par
                wait(sp, xnt_ready, c - 1)
                sp.dma_start(xh[:, par], xhat_d[bass.ds(c, 1)].rearrange("a p d -> (a p) d")).then_inc(xhat_loaded[par], 16)
                if not lead or par == 1:
                    if not lead:
                        store_gc(i - 1, par)
                    store_q(i if par else i - 1, 1 - par)

            def blocks(i, par, which, s):
                dst = (pbd, sbd)[which]
                for a in range(2):
                    lo = HD * a + HALF * which
                    sp.dma_start(dst[lo:lo + HALF, par, :, lo:lo + HALF],
                                 inv_d[which][bass.ds(2 * i + par, 1), :, a].rearrange("c h i j -> (c i) h j")
                                 ).then_inc(s, 16)

            def load_gram(i, par, s):
                src = gc_d[bass.ds(2 * i + par, 1)].rearrange("c h r n -> (c r) h n")
                sp.dma_start(gct[:, par], src).then_inc(s, 16)
                for a in range(2):
                    sl = slice(HD * a, HD * (a + 1))
                    sp.dma_start(gbd[sl, par, :, sl], src[sl, :, 0:HD]).then_inc(s, 16)

            def store_schur(i, par):
                wait(sp, schur_copied, 2 * i + par + 1)
                sp.dma_start(schur_d[bass.ds(2 * i + par, 1)].rearrange("c p n -> (c p) n"), sch[:, par]
                             ).then_inc(schur_stored[par], 16)

            def load_schur(i, v):
                for par in range(2):
                    c = 2 * i + par
                    wait(sp, t_ready, c - 1)
                    wait(sp, schur_ready, c - 3)
                    sp.dma_start(gct[:, par, :, schur_columns(v)], gc_d[bass.ds(c, 1), :, :, HALF:HD].rearrange(
                        "c h r n -> (c r) h n")).then_inc(blocks_loaded[par], 16)
                    blocks(i, par, 0, blocks_loaded[par])

            def solve(i, par):
                c = 2 * i + par
                wait(sp, w_ready, c - 1)
                wait(sp, r2_done, c - 1)
                load_gram(i, par, solve_loaded[par])
                blocks(i, par, 0, solve_loaded[par])
                blocks(i, par, 1, solve_loaded[par])

            def store_factors(i, par):
                c = 2 * i + par
                wait(sp, yt_copied, c + 1)
                sp.dma_start(yt_d[bass.ds(c, 1)].rearrange("a r n -> (a r) n"), yts[:, par]).then_inc(factors_stored[par], 16)
                wait(sp, z_copied, c + 1)
                sp.dma_start(z_d[bass.ds(c, 1)].rearrange("a r n -> (a r) n"), zs[:, par]).then_inc(factors_stored[par], 16)
                wait(sp, m_copied, c + 1)
                for a in range(2):
                    sl = slice(RANK * a, RANK * (a + 1))
                    sp.dma_start(m_d[bass.ds(2 * c + a, 1)].rearrange("a h r n -> (a r) h n"),
                                 ms[sl, par].rearrange("r (h n) -> r h n", h=PAIRS)[:, :, sl]).then_inc(factors_stored[par], 16)

            def load_apply(i, par):
                c = 2 * i + par
                wait(sp, ot_ready, 2 * (c - 1))
                wait(sp, x2_done, c - 1)
                s = apply_loaded[par]
                sp.dma_start(zl[:, par].rearrange("r (g u) n -> r g (u n)", g=4),
                             z_d[bass.ds(c, 1)].rearrange("a (g r) n -> (a r) g n", g=4)[0:2 * RANK]
                             ).then_inc(s, 16)
                sp.dma_start(ytl[:, par].rearrange("r (g u) n -> r g (u n)", g=4),
                             yt_d[bass.ds(c, 1)].rearrange("a (g r) n -> (a r) g n", g=4)[0:2 * RANK]
                             ).then_inc(s, 16)
                for a in range(2):
                    lo = RANK * a
                    sp.dma_start(mbd[lo:lo + RANK, par, :, lo:lo + RANK],
                                 minv_d[bass.ds(2 * c + a, 1)].rearrange("a h i j -> (a i) h j")).then_inc(s, 16)
                sp.dma_start(qt[:, par], q_d[bass.ds(c, 1)].rearrange("a p h r -> (a p) h r")).then_inc(s, 16)
                sp.dma_start(resl[:, par], res_d[bass.ds(c, 1)].rearrange("a p d -> (a p) d")).then_inc(s, 16)

            def store_out(i, par):
                c = 2 * i + par
                wait(sp, o_done, c + 1)
                sp.dma_start(out_chunks[bass.ds(c, 1)].rearrange("a p d -> (a p) d"), yo[:, par]).then_inc(out_stored[par], 16)

            def project_all(b):
                first, last = PAIRS_B * b, PAIRS_B * (b + 1)
                sp.wait_ge(ln_stored[2 * b], 32)
                for par in range(2):
                    project(first, par, True)
                for par in range(2):
                    project(first + 1, par, False)
                sp.wait_ge(ln_stored[2 * b + 1], 32)
                with sp.Fori(first + 2, last) as i:
                    for par in range(2):
                        project(i, par, False)
                store_gc(last - 1, 0)
                store_q(last - 1, 1)
                store_gc(last - 1, 1)

            def schur_all(b, solved):
                first, last = PAIRS_B * b, PAIRS_B * (b + 1)
                for n in range(2):
                    sp.wait_ge(gc_stored[n], 16 * last)
                sp.wait_ge(inv_stored[SWEEPS.index((0, b))], 16)
                wait(sp, w_ready, solved)
                wait(sp, r2_done, solved)
                load_schur(first, 0)
                for i in range(first + 1, last):
                    load_schur(i, i % 2)
                    for par in range(2):
                        store_schur(i - 1, par)
                for par in range(2):
                    store_schur(last - 1, par)

            def solve_inputs(n):
                if n % PAIRS_B == 0 and n < ALL_PAIRS:
                    for k in range(2):
                        sp.wait_ge(inv_stored[SWEEPS.index((k, n // PAIRS_B))], 64 if k else 16)

            def apply_inputs(n):
                if n >= LAG and (n - LAG) % PAIRS_B == 0:
                    sp.wait_ge(minv_stored[(n - LAG) // PAIRS_B], 16)
                    if n == LAG:
                        for m in range(2):
                            sp.wait_ge(q_stored[m], 16 * NCH // 2)

            def fused(lo, hi, projected, formed):
                sp.wait_ge(schur_ready, formed)
                for n in range(2):
                    sp.wait_ge(gc_stored[n], 8 * projected)

                def loads(i, par, has_a, has_b):
                    if has_a:
                        solve(i, par)
                    if has_b:
                        load_apply(i - LAG, par)

                def stores(i, par, has_a, has_e):
                    if has_a:
                        store_factors(i, par)
                    if has_e:
                        store_out(*((i - LAG, 0) if par else (i - LAG - 1, 1)))

                n = lo
                while n < hi:
                    solve_inputs(n)
                    apply_inputs(n)
                    cuts = [c for c in range(n + 1, hi) if c in CUTS or c % PAIRS_B == 0 or (c - LAG) % PAIRS_B == 0
                            or c == ALL_PAIRS + 1 or c == lo + 1]
                    stop = min(cuts + [hi])
                    has_a, has_b = n < ALL_PAIRS, n >= LAG

                    def pair(i):
                        loads(i, 0, has_a, has_b)
                        if n > lo:
                            stores(i - 1, 1, n <= ALL_PAIRS, n - 1 >= LAG)
                        loads(i, 1, has_a, has_b)
                        stores(i, 0, has_a, n > LAG)

                    if stop - n == 1:
                        pair(n)
                    else:
                        with sp.Fori(n, stop) as i:
                            pair(i)
                    n = stop
                stores(hi - 1, 1, hi - 1 < ALL_PAIRS, hi - 1 >= LAG)

            def joint(lo, hi, projected, formed):
                sp.wait_ge(schur_ready, formed)
                for g in range(2):
                    sp.wait_ge(ln_stored[2 * (BATCH - 1) + g], 32)
                solve_inputs(lo)

                def loads(i, par):
                    solve(i, par)
                    c = 2 * (i + BESIDE) + par
                    wait(sp, xnt_ready, c - 1)
                    sp.dma_start(xh[:, par], xhat_d[bass.ds(c, 1)].rearrange("a p d -> (a p) d")).then_inc(xhat_loaded[par], 16)

                def stores(i, par, lead):
                    if not lead:
                        store_gc(*((i + BESIDE, 0) if par else (i + BESIDE - 1, 1)))
                    store_factors(i, par)
                    store_q(i + BESIDE, par)

                loads(lo, 0)
                loads(lo, 1)
                stores(lo, 0, True)
                loads(lo + 1, 0)
                stores(lo, 1, False)
                loads(lo + 1, 1)
                stores(lo + 1, 0, False)
                with sp.Fori(lo + 2, hi) as i:
                    loads(i, 0)
                    stores(i - 1, 1, False)
                    loads(i, 1)
                    stores(i, 0, False)
                stores(hi - 1, 1, False)
                store_gc(hi + BESIDE - 1, 1)

            sp.wait_ge(zeroed, 12)
            projected = formed = solved = 0
            for stage, *at in merged(PROGRAM):
                if stage == "project":
                    project_all(*at)
                    projected += CPB
                elif stage == "schur":
                    schur_all(*at, solved)
                    formed += CPB
                elif stage == "joint":
                    joint(*at, projected, formed)
                    projected += CPB
                    solved = 2 * at[1]
                elif stage == "fused":
                    fused(*at, projected, formed)
                    solved = 2 * min(at[1], ALL_PAIRS)
            store_out(*LAST)
            for n in range(2):
                sp.wait_ge(out_stored[n], 16 * NCH // 2)
                sp.wait_ge(factors_stored[n], 64 * NCH // 2)

        @block.gpsimd
        def _(pool):
            nc.gpsimd.memset(ident[:], 0.0).then_inc(zeroed, 1)
            pool.wait_ge(zeroed, 1)
            nc.gpsimd.affine_select(out=ident[:], in_=ident[:], compare_op=ALU.not_equal, fill=1.0, base=0,
                                    pattern=[[-1, P]], channel_multiplier=1).then_inc(zeroed, 1)
            nc.gpsimd.memset(half_neg[:], -0.5).then_inc(zeroed, 1)
            nc.gpsimd.memset(ones[:], 1.0).then_inc(zeroed, 1)
            for g in range(2):
                pool.dma_start(xg[:, g], x_groups[g]).then_inc(x_loaded[g], 16)
            for t in (gbd, pbd, sbd, wbd, we, mbd, state, xs):
                nc.gpsimd.memset(t[:], 0.0).then_inc(zeroed, 1)

            for g in range(NCH // GROUP):
                pool.wait_ge(veps_ready, 2 * g + 1)
                nc.gpsimd.tensor_tensor(rstd[:], veps[:], half_neg[:], ALU.pow).then_inc(rstd_ready, 1)
                pool.wait_ge(veps_ready, 2 * g + 2)
                nc.gpsimd.tensor_tensor(rstd2[:], veps2[:], half_neg[:], ALU.pow).then_inc(rstd_ready, 1)
                pool.wait_ge(hat_ready, g + 1)
                chunks = slice(g * GROUP, (g + 1) * GROUP)
                pool.dma_start(xhat_d[chunks].rearrange("k p d -> p k d"), hatg[:, g % 2]).then_inc(ln_stored[g], 16)
                pool.dma_start(res_d[chunks].rearrange("k p d -> p k d"), lng[:, g % 2]).then_inc(ln_stored[g], 16)
                if g + 2 < NCH // GROUP:
                    pool.dma_start(xg[:, g % 2], x_groups[g + 2]).then_inc(x_loaded[g % 2], 16)

            def load(k):
                which, b = SWEEPS[k]
                chunks = slice(CPB * b, CPB * (b + 1))
                for n in range(2):
                    pool.wait_ge((gc_stored, schur_stored)[which][n], 16 * PAIRS_B * (b + 1))
                if k >= 2:
                    pool.wait_ge(mirrored, 3 * (k - 1))
                dst = work[:, 2 * (k % 2), :].rearrange("p (i j) -> p i j", i=HALF)
                if which == 0:
                    src = gc_d[chunks, :, :, 0:HALF].rearrange("c h (s r) n -> (c h s) r n", s=2)[:, 0:HALF]
                    pool.dma_start(dst, src).then_inc(sweep_loaded[k % 2], 16)
                else:
                    for g in range(4):
                        pool.dma_start(dst[HALF * g:HALF * (g + 1)],
                                       schur_d[chunks].rearrange("c (a i) n -> (c a) i n", i=HALF)
                                       [:, :, HALF * g:HALF * (g + 1)]).then_inc(sweep_loaded[k % 2], 16)

            def finish(k):
                which, b = SWEEPS[k]
                pool.wait_ge(inverted, k + 1)
                if k >= 1:
                    pool.wait_ge(inv_stored[k - 1], 64 if SWEEPS[k - 1][0] else 16)
                src = work[:, 2 * (k % 2), :].rearrange("p (i j) -> p i j", i=HALF)
                nc.gpsimd.affine_select(out=upper[:], in_=src, compare_op=ALU.is_ge, fill=0.0, base=0,
                                        pattern=[[-1, HALF], [1, HALF]], channel_multiplier=0).then_inc(mirrored, 1)
                nc.gpsimd.affine_select(out=lower[:], in_=src.rearrange("p i j -> p j i"), compare_op=ALU.is_gt,
                                        fill=0.0, base=0, pattern=[[1, HALF], [-1, HALF]],
                                        channel_multiplier=0).then_inc(mirrored, 1)
                pool.wait_ge(mirrored, 3 * k + 2)
                nc.gpsimd.tensor_tensor(upper[:], upper[:], lower[:], ALU.add).then_inc(mirrored, 1)
                pool.wait_ge(mirrored, 3 * k + 3)
                if which == 0:
                    pool.dma_start(inv_d[0][CPB * b:CPB * (b + 1)].rearrange("c h s i j -> (c h s) (i j)"),
                                   upper[:].rearrange("p i j -> p (i j)")).then_inc(inv_stored[k], 16)
                else:
                    for g in range(4):
                        pool.dma_start(inv_d[1][CPB * b:CPB * (b + 1), 2 * g:2 * g + 2].rearrange(
                            "c u s i j -> c (u s) (i j)"), upper[HALF * g:HALF * (g + 1)].rearrange("p i j -> p (i j)")
                                       ).then_inc(inv_stored[k], 16)

            pool.wait_ge(sgn_copied, 8)
            def norm3(i, par):
                c = 2 * i + par
                wait(pool, ve3_ready, c + 1)
                nc.gpsimd.tensor_tensor(rs3[:], ve3[:], half_neg[:, 0:1], ALU.pow).then_inc(rs3_ready, 1)

            def small_load(b):
                for n in range(2):
                    pool.wait_ge(factors_stored[n], 64 * PAIRS_B * (b + 1))
                if b:
                    pool.wait_ge(minv_stored[b - 1], 16)
                pool.dma_start(msw[:, 0], m_d[2 * CPB * b:2 * CPB * (b + 1)].rearrange("c h i j -> (c h) i j")
                               ).then_inc(m_loaded, 16)

            def small_finish(b):
                pool.wait_ge(m_inverted, b + 1)
                pool.dma_start(minv_d[2 * CPB * b:2 * CPB * (b + 1)].rearrange("c h i j -> (c h) (i j)"),
                               msw[:, 0].rearrange("p i j -> p (i j)")).then_inc(minv_stored[b], 16)

            swept_so_far = [0] * len(SWEEPS)

            def advance(k, pivots):
                swept_so_far[k] += pivots
                if swept_so_far[k] == HALF:
                    finish(k)

            def norm(a, b, e):
                if b:
                    norm3(*b)

            for stage, *at in PROGRAM:
                if stage == "load":
                    load(*at)
                elif stage == "sweep":
                    advance(*at)
                elif stage == "joint":
                    lo, hi, k, pivots = at
                    advance(k, 2 * (hi - lo) * pivots)
                elif stage == "fused":
                    lo, hi, k, pivots, small = at
                    if small is None:
                        if lo >= LAG:
                            fused_pairs(pool, lo, hi, norm)
                    else:
                        small_load(small)
                        if lo >= LAG:
                            norm3(lo - LAG, 0)
                        small_finish(small)
                        if lo >= LAG:
                            norm3(lo - LAG, 1)
                    if k is not None:
                        advance(k, 2 * (hi - lo) * pivots)

        @block.scalar
        def _(act):
            act.wait_ge(ffw_loaded, 32)
            for t in range(FT):
                if t:
                    act.wait_ge(abs_done, t)
                nc.scalar.activation(absw[:, 0:DM], w1n[:, t], ACT.Abs, accum_out=alpha1[:, t:t + 1]).then_inc(abs_done, 1)
            for t in range(KT):
                act.wait_ge(abs_done, FT + t)
                nc.scalar.activation(absw, w2n[:, t], ACT.Abs, accum_out=alpha2[:, t:t + 1]).then_inc(abs_done, 1)
            act.wait_ge(abs_done, FT + KT)
            nc.scalar.activation(w1n, w1n, ACT.Sign).then_inc(sign_done, 1)
            nc.scalar.activation(w2n, w2n, ACT.Sign).then_inc(sign_done, 1)
            nc.scalar.mul(alpha1[:], alpha1[:], 1.0 / DM).then_inc(alpha_done, 1)
            nc.scalar.mul(alpha2[:], alpha2[:], 1.0 / FF).then_inc(alpha_done, 1)
            act.wait_ge(alpha_done, 2)
            act.wait_ge(zeroed, 2)
            for t in range(KT):
                nc.scalar.activation(diag[:, t], ident[:], ACT.Copy, scale=alpha2[:, t:t + 1]).then_inc(diag_done, 1)
            for n in range(8):
                act.wait_ge(sgn_ready, n + 1)
                if n < 4:
                    dst = s1t[:, n // 2, (n % 2) * BANK:(n % 2 + 1) * BANK]
                else:
                    dst = s2t[:, 2 * (n - 4):2 * (n - 3)].rearrange("p t d -> p (t d)")
                nc.scalar.copy(dst, bank[n][:]).then_inc(sgn_copied, 1)
            act.wait_ge(alpha_bcast, 1)
            nc.scalar.copy(alpha2r[:], bank[0][:, 0:DM]).then_inc(alpha_row, 1)

            nc.scalar.copy(ident16[:], ident[:]).then_inc(ident16_done, 1)

            act.wait_ge(consts_loaded, 48)

            def copy_gc(i, par):
                c = 2 * i + par
                wait(act, gc_stored[par], 16 * i)
                for j in range(2):
                    wait(act, gc_ready, 2 * c + j + 1)
                    nc.scalar.copy(gc[:, par, 4 * j:4 * j + 4].rearrange("p h n -> p (h n)"), bank[4 + j][:]
                                   ).then_inc(gc_copied, 1)

            def project(i, par, lead):
                c = 2 * i + par
                wait(act, xnt_ready, c + 1)
                for t in range(KT):
                    ins = nc.scalar.activation(xnt[:, par, t], bank[0][:, P * t:P * (t + 1)], ACT.Identity,
                                               scale=gain[:, t:t + 1], bias=bias[:, t:t + 1])
                ins.then_inc(xnt_copied, 1)
                if not lead or par == 1:
                    copy_gc(i if par else i - 1, 1 - par)
                for n in range(6):
                    if n == 4:
                        wait(act, q_stored[par], 16 * i)
                    wait(act, kvq_ready, 6 * c + n + 1)
                    if n < 4:
                        dst = kv[:, par, n // 2, (n % 2) * BANK:(n % 2 + 1) * BANK]
                    else:
                        dst = qt[:, par, 4 * (n - 4):4 * (n - 3)].rearrange("p h r -> p (h r)")
                    nc.scalar.copy(dst, bank[1 + n % 3][:]).then_inc(kvq_copied, 1)

            def schur(i, v):
                for par in range(2):
                    wait(act, t_ready, 2 * i + par + 1)
                    nc.scalar.copy(tts[:, par], bank[6 + par][:, 0:2 * P]).then_inc(t_copied, 1)
                for par in range(2):
                    wait(act, turned_ready, 2 * i + par + 1)
                    for s in range(2):
                        sl = slice(HD * s, HD * s + HALF)
                        ins = nc.scalar.copy(xs[sl, par, :, :, HALF * s:HALF * (s + 1)].rearrange("p u g j -> p (u g) j"),
                                             bank[6 + par][sl, 2 * P:4 * P].rearrange("p (a j) -> p a j", j=HALF))
                    ins.then_inc(turned_copied, 1)
                for par in range(2):
                    wait(act, schur_ready, 2 * i + par + 1)
                    wait(act, schur_stored[par], 16 * i)
                    nc.scalar.copy(sch[:, par], bank[6 + par][:, 0:2 * HD]).then_inc(schur_copied, 1)

            def project_step(i, par, lead, n):
                c = 2 * i + par
                if n == 0:
                    wait(act, xnt_ready, c + 1)
                    for t in range(KT):
                        ins = nc.scalar.activation(xnt[:, par, t], bank[5][:, P * t:P * (t + 1)], ACT.Identity,
                                                   scale=gain[:, t:t + 1], bias=bias[:, t:t + 1])
                    ins.then_inc(xnt_copied, 1)
                elif n in (3, 6):
                    if not lead:
                        j = n // 3 - 1
                        wait(act, gc_stored[1 - par], 16 * (i if par else i - 1))
                        wait(act, gc_ready, 2 * c - 1 + j)
                        nc.scalar.copy(gc[:, 1 - par, 4 * j:4 * j + 4].rearrange("p h n -> p (h n)"), bank[5][:]
                                       ).then_inc(gc_copied, 1)
                else:
                    m = PRODUCT_STEPS.index(n)
                    if m == 4:
                        wait(act, q_stored[par], 16 * i)
                    wait(act, kvq_ready, 6 * c + m + 1)
                    if m < 4:
                        dst = kv[:, par, m // 2, (m % 2) * BANK:(m % 2 + 1) * BANK]
                    else:
                        dst = qt[:, par, 4 * (m - 4):4 * (m - 3)].rearrange("p h r -> p (h r)")
                    nc.scalar.copy(dst, bank[6 + m % 2][:]).then_inc(kvq_copied, 1)

            def chunk(a, b, e, step=lambda n: None):
                def flat(t):
                    return t.rearrange("p h n -> p (h n)")
                if a:
                    i, par = a
                    c = 2 * i + par
                if b:
                    j, q = b
                    d = 2 * j + q
                if e:
                    f = 2 * e[0] + e[1]

                def copy_nz():
                    wait(act, nz_ready, d + 1)
                    nc.scalar.mul(flat(nz[:]), bank[NZ_BANK[not a]][0:2 * RANK, :], -1.0).then_inc(nz_copied, 1)

                def gelu(n):
                    for t in range(4 * n, 4 * n + 4):
                        if t % 4 == 0:
                            wait(act, h_ready, 2 * f + n + 1)
                        nc.scalar.activation(ht[:, t], bank[6 + n][:, P * (t % 4):P * (t % 4 + 1)], ACT.Gelu,
                                             scale=alpha1[:, t:t + 1], bias=b1c[:, t:t + 1]).then_inc(h_copied, 1)

                def high(n):
                    act.wait_ge(h_copied, FT * f + 4 * n + 4)
                    nc.scalar.copy(hsplit[:, 0, 4 * n:4 * n + 4], ht[:, 4 * n:4 * n + 4]).then_inc(high_done, 1)

                if a:
                    wait(act, y_ready, c + 1)
                    nc.scalar.copy(flat(ysb[:]), bank[0][:]).then_inc(y_copied, 1)
                step(0)
                step(1)
                if b and not a:
                    copy_nz()
                if e:
                    wait(act, y3t_ready, f + 1)
                    nc.scalar.copy(y3t[:].rearrange("p a t r -> p (a t r)"), bank[5][:]).then_inc(y3t_copied, 1)
                    gelu(0)
                if a:
                    wait(act, w2_ready, c + 1)
                    nc.scalar.copy(flat(w2sb[:]), bank[2][:]).then_inc(w2_copied, 1)
                step(2)
                step(3)
                if e:
                    high(0)
                    gelu(1)
                    high(1)
                if a and b:
                    copy_nz()
                if a:
                    wait(act, w_ready, c + 1)
                    for s in range(2):
                        sl = slice(HD * s, HD * (s + 1))
                        nc.scalar.mul(wbd[sl, :, sl], bank[2][sl, :].rearrange("p (h n) -> p h n", n=HD), -1.0
                                      ).then_inc(wbd_copied, 1)
                    for s in range(2):
                        sl = slice(HD * s, HD * (s + 1))
                        nc.scalar.mul(we[sl, :, RANK * s:RANK * (s + 1)],
                                      bank[2][sl, :].rearrange("p (h n) -> p h n", n=HD)[:, :, 0:RANK], -1.0)
                    nc.scalar.mul(flat(wt[:]), bank[2][:], -1.0).then_inc(w_copied, 1)
                step(4)
                if a:
                    for n in range(2):
                        wait(act, wbdt_ready, 2 * c + n + 1)
                        nc.scalar.copy(flat(wbdt[:, 4 * n:4 * n + 4]), bank[3 + n][:]).then_inc(wbdt_copied, 1)
                step(5)
                if b:
                    for n in range(2):
                        wait(act, ot_ready, 2 * d + n + 1)
                        nc.scalar.mul(ot[:, 4 * n:4 * n + 4].rearrange("p h r -> p (h r)"), bank[OT_BANKS[not a][n]][:],
                                      SCALE).then_inc(ot_copied, 1)
                if a:
                    wait(act, yt_ready, c + 1)
                    wait(act, factors_stored[par], 64 * i)
                    nc.scalar.copy(yts[:, par], bank[0][:, 0:2 * P]).then_inc(yt_copied, 1)
                step(6)
                if a:
                    wait(act, y2_ready, c + 1)
                    nc.scalar.copy(flat(y2bd[:]), bank[1][:, 0:2 * P]).then_inc(y2_copied, 1)
                step(7)
                if a:
                    wait(act, z_ready, c + 1)
                    nc.scalar.copy(zs[:, par], bank[3][:, 0:2 * HD]).then_inc(z_copied, 1)
                    wait(act, m_ready, c + 1)
                    nc.scalar.copy(ms[:, par], bank[4][0:2 * RANK, 0:2 * RANK * PAIRS]).then_inc(m_copied, 1)
                step(8)

            def project_all(b):
                first, last = PAIRS_B * b, PAIRS_B * (b + 1)
                for par in range(2):
                    project(first, par, True)
                with act.Fori(first + 1, last) as i:
                    for par in range(2):
                        project(i, par, False)
                copy_gc(last - 1, 1)

            for stage, *at in merged(PROGRAM):
                if stage == "project":
                    project_all(*at)
                elif stage == "schur":
                    if at[0] == 0:
                        for g in range(NCH // GROUP):
                            act.wait_ge(ln_stored[g], 32)
                        act.wait_ge(zeroed, 12)
                        for par in range(2):
                            for s in range(2):
                                sl = slice(HD * s + HALF, HD * (s + 1))
                                nc.scalar.copy(xs[sl, par, :, :, HALF * s:HALF * (s + 1)].rearrange("p u g j -> p (u g) j"),
                                               ident[sl, sl].unsqueeze(1).broadcast_to([HALF, PAIRS, HALF])
                                               ).then_inc(eye_placed, 1)
                    each_two_pairs(act, at[0], schur)
                elif stage == "joint":
                    lo, hi = at

                    def beside(solved, attended, fed, lead=False):
                        i, par = solved
                        chunk(solved, None, None, lambda n: project_step(i + BESIDE, par, lead, n))

                    for par in range(2):
                        beside((lo, par), None, None, par == 0)
                    fused_pairs(act, lo + 1, hi, beside)
                    last = hi + BESIDE
                    act.wait_ge(gc_stored[1], 16 * (last - 1))
                    for j in range(2):
                        act.wait_ge(gc_ready, 4 * last - 1 + j)
                        nc.scalar.copy(gc[:, 1, 4 * j:4 * j + 4].rearrange("p h n -> p (h n)"), bank[5][:]
                                       ).then_inc(gc_copied, 1)
                elif stage == "fused":
                    fused_pairs(act, *at, chunk)
            chunk(None, None, LAST)

        @block.vector
        def _(dve):
            V = nc.vector
            dve.wait_ge(zeroed, 4)
            step = [0]

            def link(ins):
                step[0] += 1
                ins.then_inc(ln_step, 1)

            def settle():
                dve.wait_ge(ln_step, step[0])

            def statistics(src, moments, var_eps):
                for k in range(GROUP):
                    link(V.bn_stats(stats[:, k], src[:, k]))
                settle()
                for k in range(GROUP):
                    link(V.bn_aggr(moments[:, k], stats[:, k]))
                settle()
                V.tensor_scalar(var_eps, moments[:, :, 1], LN_EPS, None, ALU.add).then_inc(veps_ready, 1)

            for g in range(NCH // GROUP):
                n = g % 2
                dve.wait_ge(x_loaded[n], 16 * (g // 2 + 1))
                statistics(xg[:, n], mv, veps[:])
                if g >= 2:
                    dve.wait_ge(ln_stored[g - 2], 32)
                dve.wait_ge(rstd_ready, 2 * g + 1)
                for k in range(GROUP):
                    link(V.tensor_scalar(lng[:, n, k], xg[:, n, k], mv[:, k, 0:1], rstd[:, k:k + 1],
                                         ALU.subtract, ALU.mult))
                settle()
                statistics(lng[:, n], mv2, veps2[:])
                dve.wait_ge(rstd_ready, 2 * g + 2)
                for k in range(GROUP):
                    link(V.tensor_scalar(hatg[:, n, k], lng[:, n, k], mv2[:, k, 0:1], rstd2[:, k:k + 1],
                                         ALU.subtract, ALU.mult))
                settle()
                V.tensor_tensor(lng[:, n], lng[:, n], xg[:, n], ALU.add).then_inc(hat_ready, 1)

            done = [0]

            def pivot(src, dst, size, strips, count, wait_first):
                n = size
                if wait_first is not None:
                    dve.wait_ge(swept, wait_first)
                V.reciprocal(piv[:], src[:, 0, 0:1]).then_inc(swept, 1)
                dve.wait_ge(swept, count + 1)
                V.tensor_scalar(prow[:, 1:n], src[:, 0, 1:n], piv[:], None, ALU.mult).then_inc(swept, 1)
                V.tensor_scalar(dst[:, 0:n - 1, n - 1], src[:, 0, 1:n], piv[:], None, ALU.mult).then_inc(swept, 1)
                V.tensor_scalar(dst[:, n - 1, n - 1:n], piv[:], -1.0, None, ALU.mult).then_inc(swept, 1)
                dve.wait_ge(swept, count + 2)
                at = 0
                tiles = []
                for r0, r1 in strips:
                    rows, cols = r1 - r0, n - 1 - r0
                    t = outer[:, at:at + rows * cols].rearrange("p (i j) -> p i j", i=rows)
                    at += rows * cols
                    tiles.append(t)
                    V.tensor_tensor(t, src[:, 0, r0 + 1:r1 + 1].unsqueeze(2).broadcast_to([P, rows, cols]),
                                    prow[:, r0 + 1:n].unsqueeze(1).broadcast_to([P, rows, cols]), ALU.mult).then_inc(swept, 1)
                for m, (r0, r1) in enumerate(strips):
                    dve.wait_ge(swept, count + 4 + m + 1)
                    V.tensor_tensor(dst[:, r0:r1, r0:n - 1], src[:, r0 + 1:r1 + 1, r0 + 1:n], tiles[m],
                                    ALU.subtract).then_inc(swept, 1)

            STRIPS = [(0, 16), (16, 31)]
            PER = 4 + 2 * len(STRIPS)

            def square(k, n):
                return work[:, 2 * (k % 2) + n, :].rearrange("p (i j) -> p i j", i=HALF)

            def begin(k):
                dve.wait_ge(sweep_loaded[k % 2], 16 * sum(4 if SWEEPS[m][0] else 1 for m in range(k % 2, k + 1, 2)))
                dg = work[:, 2 * (k % 2), 0:HALF * HALF:HALF + 1]
                V.tensor_scalar(dg, dg, RIDGE, None, ALU.add).then_inc(swept, 1)
                if k < 2:
                    V.memset(square(k, 1)[:], 0.0).then_inc(swept, 1)
                    done[0] += 1
                done[0] += 1

            pivoted = [0] * len(SWEEPS)

            def pivots_of(k, first, number, count):
                for t in range(number):
                    n = (first + t) % 2
                    pivot(square(k, n), square(k, 1 - n), HALF, STRIPS, count + t * PER, count + t * PER)

            def advance(k, number):
                pivoted[k] += number
                if pivoted[k] == HALF:
                    dve.wait_ge(swept, done[0])
                    V.tensor_copy(piv[:], piv[:]).then_inc(inverted, 1)
                    dve.wait_ge(inverted, k + 1)

            def sweep(k, number):
                if pivoted[k] == 0:
                    begin(k)
                base = done[0]
                with dve.Fori(0, number // 2) as t:
                    pivots_of(k, 0, 2, t * (2 * PER) + base)
                done[0] += number * PER
                advance(k, number)

            def small_sweep(b, half):
                a, z = msw[:, 0], msw[:, 1]
                strips = [(0, RANK - 1)]
                per = 4 + 2 * len(strips)
                if half == 0:
                    dve.wait_ge(m_loaded, 16 * (b + 1))
                    V.memset(z[:], 0.0).then_inc(swept, 1)
                    done[0] += 1
                for t in range(RANK // 2 * half, RANK // 2 * (half + 1)):
                    src, dst = (a, z) if t % 2 == 0 else (z, a)
                    pivot(src, dst, RANK, strips, done[0], done[0])
                    done[0] += per
                if half == 1:
                    dve.wait_ge(swept, done[0])
                    for r in range(1, RANK):
                        V.tensor_copy(a[:, r, 0:r], a[:, 0:r, r]).then_inc(swept, 1)
                    done[0] += RANK - 1
                    dve.wait_ge(swept, done[0])
                    V.tensor_copy(piv[:], piv[:]).then_inc(m_inverted, 1)
                    dve.wait_ge(m_inverted, b + 1)

            def chunk(a, b, e, slot):
                def banked(n, width):
                    return bank[n][:].rearrange("p (h n) -> p h n", n=width)
                if b:
                    j, q = b
                    d = 2 * j + q

                def decay():
                    wait(dve, wr_ready, d + 1)
                    for s in range(2):
                        sl = slice(HD * s, HD * (s + 1))
                        V.scalar_tensor_tensor(out=state[sl, q, :, sl], in0=state[sl, 1 - q, :, sl], scalar=DECAY,
                                               in1=banked(WR_BANK[not a], HD)[sl], op0=ALU.mult, op1=ALU.add
                                               ).then_inc(state_done, 1)

                if b and not a:
                    decay()
                if a:
                    i, par = a
                    c = 2 * i + par
                    wait(dve, g1_ready, c + 1)
                    V.tensor_tensor(rsb[:], banked(1, HD), gct[:, par, :, HD:2 * HD], ALU.add).then_inc(r1_done, 1)
                slot(0)
                if a:
                    wait(dve, g2_ready, c + 1)
                    V.tensor_tensor(r2sb[:], banked(1, HD), gct[:, par, :, HD:2 * HD], ALU.add).then_inc(r2_done, 1)
                if e:
                    f = 2 * e[0] + e[1]
                    for n in range(2):
                        wait(dve, high_done, 2 * f + n + 1)
                        V.tensor_tensor(hsplit[:, 1, 4 * n:4 * n + 4], ht[:, 4 * n:4 * n + 4], hsplit[:, 0, 4 * n:4 * n + 4],
                                        ALU.subtract).then_inc(low_done, 1)
                slot(1)
                if a and b:
                    decay()
                if e:
                    wait(dve, o_ready, f + 1)
                    V.tensor_tensor(ysc[:], bank[5][:, 0:DM], alpha2r[:], ALU.mult).then_inc(scaled, 1)
                    wait(dve, scaled, f + 1)
                    wait(dve, x2b_done, f + 1)
                    wait(dve, out_stored[e[1]], 16 * e[0])
                    V.tensor_tensor(yo[:, e[1]], ysc[:], x2b[:], ALU.add).then_inc(o_done, 1)
                slot(2)
                if b:
                    wait(dve, wo_ready, d + 1)
                    V.tensor_tensor(x2[:], bank[5][:, 0:DM], resl[:, q], ALU.add).then_inc(x2_done, 1)
                    wait(dve, x2_done, d + 1)
                    V.bn_stats(st3[:], x2[:]).then_inc(ln3_step, 1)
                    wait(dve, ln3_step, 4 * d + 1)
                    V.tensor_tensor(unused[:], x2[:, 0:1], x2[:, 0:1], ALU.add)
                    V.bn_aggr(mv3[:], st3[:]).then_inc(ln3_step, 1)
                    wait(dve, ln3_step, 4 * d + 2)
                    V.tensor_scalar(ve3[:], mv3[:, 1:2], LN_EPS, None, ALU.add).then_inc(ve3_ready, 1)
                    V.tensor_tensor(x2b[:], x2[:], b2r[:], ALU.add).then_inc(x2b_done, 1)
                    wait(dve, rs3_ready, d + 1)
                    for part in (x3[:], x3split[:, 0]):
                        V.tensor_scalar(part, x2[:], mv3[:, 0:1], rs3[:], ALU.subtract, ALU.mult).then_inc(ln3_step, 1)
                    wait(dve, ln3_step, 4 * d + 4)
                    V.tensor_tensor(x3split[:, 1], x3[:], x3split[:, 0], ALU.subtract).then_inc(x3_ready, 1)
                slot(3)

            def fused(lo, hi, k, number, small=None):
                if lo >= LAG and (lo - LAG) % PAIRS_B == 0:
                    b = (lo - LAG) // PAIRS_B
                    wait(dve, ot_ready, 2 * CPB * b)
                    V.memset(state[:, 1], 0.0).then_inc(state_cleared, 1)
                    dve.wait_ge(state_cleared, b + 1)
                if k is not None and pivoted[k] == 0:
                    begin(k)
                base = done[0]
                each = number * PER
                spread = SLOTS[number]

                def beside(at_a, at_b, at_e):
                    pair, par = at_a or (at_b[0] + LAG, at_b[1])
                    start = (base - 2 * lo * each + par * each) + pair * (2 * each) if number else 0

                    def slot(n):
                        ahead = sum(spread[:n])
                        pivots_of(k, par * number + ahead, spread[n], start + ahead * PER)

                    def slot_with_small(n):
                        if spread[n]:
                            pivots_of(k, par * number + sum(spread[:n]), spread[n], done[0])
                            done[0] += spread[n] * PER
                        if par == 0 and n in (1, 2):
                            small_sweep(small, n - 1)

                    chunk(at_a, at_b, at_e, slot if small is None else slot_with_small)

                fused_pairs(dve, lo, hi, beside)
                if small is None:
                    done[0] += 2 * (hi - lo) * each
                if k is not None:
                    advance(k, 2 * (hi - lo) * number)

            ready = False
            for stage, *at in PROGRAM:
                if stage == "sweep":
                    sweep(*at)
                elif stage in ("joint", "fused"):
                    if not ready:
                        dve.wait_ge(alpha_row, 1)
                        dve.wait_ge(zeroed, 12)
                        dve.wait_ge(b2_loaded, 16)
                        ready = True
                    fused(*at)
            chunk(None, None, LAST, lambda n: None)

        @block.tensor
        def _(pe):
            mm = nc.tensor.matmul
            pe.wait_ge(zeroed, 2)
            pe.wait_ge(sign_done, 2)
            for n in range(8):
                for t in range(4):
                    if n < 4:
                        src = w1n[:, 4 * (n % 2) + t, P * (n // 2):P * (n // 2 + 1)]
                    else:
                        src = w2n[:, t % 2, P * (2 * (n - 4) + t // 2):P * (2 * (n - 4) + t // 2 + 1)]
                    ins = nc.tensor.transpose(bank[n][:, P * t:P * (t + 1)], src, ident[:])
                ins.then_inc(sgn_ready, 1)
            pe.wait_ge(diag_done, 2)
            pe.wait_ge(zeroed, 4)
            pe.wait_ge(sgn_copied, 8)
            mm(bank[0][:, 0:DM], ones[:], diag[:].rearrange("p t d -> p (t d)"), start=True, stop=True).then_inc(alpha_bcast, 1)
            pe.wait_ge(alpha_row, 1)
            pe.wait_ge(qkv_loaded, 64)

            def half_gram(par, j, dst):
                for h in range(8 * j, 8 * j + 8):
                    cols = slice(HD * h, HD * (h + 1))
                    lo = HD * (h % 2)
                    at = 2 * HD * (h // 2 % 4)
                    ins = mm(dst[lo:lo + HD, at:at + 2 * HD], kv[:, par, 0, cols], kv[:, par, :, cols], start=True, stop=True)
                ins.then_inc(gc_ready, 1)

            def product(par, n, dst):
                if n < 4:
                    for t in range(KT):
                        ins = mm(dst[:], xnt[:, par, t], wqkv[:, n // 2, t, (n % 2) * BANK:(n % 2 + 1) * BANK],
                                 start=t == 0, stop=t == KT - 1)
                else:
                    for h in range(4):
                        cols = slice(P * (4 * (n - 4) + h), P * (4 * (n - 4) + h + 1))
                        for t in range(KT):
                            ins = mm(dst[:, P * h:P * (h + 1)], wqkv[:, 2, t, cols], xnt[:, par, t],
                                     start=t == 0, stop=t == KT - 1)
                ins.then_inc(kvq_ready, 1)

            def gram(i, par):
                c = 2 * i + par
                wait(pe, kvq_copied, 6 * c + 4)
                for j in range(2):
                    wait(pe, gc_copied, 2 * c + j - 1)
                    half_gram(par, j, bank[4 + j])

            def project(i, par, lead):
                c = 2 * i + par
                wait(pe, xhat_loaded[par], 16 * (i + 1))
                wait(pe, xnt_copied, c)
                for t in range(KT):
                    ins = nc.tensor.transpose(bank[0][:, P * t:P * (t + 1)], xh[:, par, P * t:P * (t + 1)], ident[:])
                ins.then_inc(xnt_ready, 1)
                if not lead or par == 1:
                    gram(i if par else i - 1, 1 - par)
                wait(pe, xnt_copied, c + 1)
                for n in range(6):
                    wait(pe, kvq_copied, 6 * c + n - 2)
                    product(par, n, bank[1 + n % 3])

            def schur(i, v):
                b_over_d = gct[:, :, :, schur_columns(v)]
                for par in range(2):
                    wait(pe, blocks_loaded[par], 48 * (i + 1))
                    wait(pe, schur_copied, 2 * i + par - 1)
                    for h in range(PAIRS):
                        o = HALF * (h // 2)
                        ins = mm(bank[6 + par][o:o + HALF, P * (h % 2):P * (h % 2 + 1)], b_over_d[:, par, h],
                                 pbd[:, par, h], start=True, stop=True)
                    ins.then_inc(t_ready, 1)
                for par in range(2):
                    wait(pe, t_copied, 2 * i + par + 1)
                    for u in range(2):
                        ins = nc.tensor.transpose(bank[6 + par][:, P * (2 + u):P * (3 + u)], tts[:, par, P * u:P * (u + 1)],
                                                  ident[:])
                    ins.then_inc(turned_ready, 1)
                for par in range(2):
                    wait(pe, turned_copied, 2 * i + par + 1)
                    for h in range(PAIRS):
                        o = HD * (h % 2)
                        ins = mm(bank[6 + par][o:o + HD, HALF * (h // 2):HALF * (h // 2 + 1)], xs[:, par, h % 2, h // 2],
                                 b_over_d[:, par, h], start=True, stop=True)
                    ins.then_inc(schur_ready, 1)

            def project_step(i, par, lead, n):
                c = 2 * i + par
                if n == 0:
                    wait(pe, xhat_loaded[par], 16 * (i + 1))
                    wait(pe, gc_copied, 2 * (c - 1))
                    for t in range(KT):
                        ins = nc.tensor.transpose(bank[5][:, P * t:P * (t + 1)], xh[:, par, P * t:P * (t + 1)], ident[:])
                    ins.then_inc(xnt_ready, 1)
                elif n in (3, 6):
                    if not lead:
                        j = n // 3 - 1
                        wait(pe, kvq_copied, 6 * c - 2)
                        wait(pe, xnt_copied, c + 1)
                        wait(pe, gc_copied, 2 * c - 2 + j)
                        half_gram(1 - par, j, bank[5])
                else:
                    m = PRODUCT_STEPS.index(n)
                    wait(pe, xnt_copied, c + 1)
                    wait(pe, kvq_copied, 6 * c + m - 1)
                    product(par, m, bank[6 + m % 2])

            def chunk(a, b, e, step=lambda n: None):
                def at(n, h, w=HD):
                    return bank[n][:, w * h:w * (h + 1)]
                if a:
                    i, par = a
                    c = 2 * i + par
                if b:
                    j, q = b
                    d = 2 * j + q
                if e:
                    f = 2 * e[0] + e[1]

                def inverse_applied():
                    wait(pe, apply_loaded[q], 96 * (j + 1))
                    if a:
                        wait(pe, h_copied, FT * d - 4)
                    else:
                        pe.wait_ge(yt_copied, NCH)
                    for h in range(PAIRS):
                        m = mbd[:, q].rearrange("p h n -> p (h n)") if h == 0 else mbd[:, q, h]
                        ins = mm(bank[NZ_BANK[not a]][0:m.shape[1], HD * h:HD * (h + 1)], m, zl[:, q, h],
                                 start=True, stop=True)
                    ins.then_inc(nz_ready, 1)

                def operator():
                    wait(pe, nz_copied, d + 1)
                    if not a:
                        pe.wait_ge(y2_copied, NCH)
                    for h in range(PAIRS):
                        ins = mm(at(WR_BANK[not a], h), ytl[:, q, h], nz[:, h], start=True, stop=True)
                    ins.then_inc(wr_ready, 1)

                def attend():
                    wait(pe, state_done, 2 * (d + 1))
                    if a:
                        wait(pe, h_copied, FT * d)
                    else:
                        pe.wait_ge(z_copied, NCH)
                        pe.wait_ge(m_copied, NCH)
                    for n in range(2):
                        for h in range(4 * n, 4 * n + 4):
                            ins = mm(bank[OT_BANKS[not a][n]][:, P * (h % 4):P * (h % 4 + 1)], state[:, q, h], qt[:, q, h],
                                     start=True, stop=True)
                        ins.then_inc(ot_ready, 1)

                def hidden(n):
                    for t in range(4 * n, 4 * n + 4):
                        for k in range(KT):
                            for part in range(2):
                                ins = mm(bank[6 + n][:, P * (t % 4):P * (t % 4 + 1)], s1t[:, k, P * t:P * (t + 1)],
                                         y3t[:, part, k], start=k + part == 0, stop=k + part == KT)
                    ins.then_inc(h_ready, 1)

                def output(n):
                    for t in range(4 * n, 4 * n + 4):
                        wait(pe, low_done, 2 * f + n + 1)
                        for part in range(2):
                            ins = mm(bank[5][:, 0:DM], hsplit[:, part, t], s2t[:, t], start=t + part == 0,
                                     stop=t + part == FT)
                    if n:
                        ins.then_inc(o_ready, 1)

                def project_out(n):
                    for h in range(4 * n, 4 * n + 4):
                        wait(pe, ot_copied, 2 * d + n + 1)
                        ins = mm(bank[5][:, 0:DM], ot[:, h], wo[:, h], start=h == 0, stop=h == PAIRS - 1)
                    if n:
                        ins.then_inc(wo_ready, 1)

                def factor(h):
                    o = 32 * (h // 2)
                    return y2bd[:, h % 2, o:o + 2 * RANK]

                if a:
                    wait(pe, solve_loaded[par], 112 * (i + 1))
                    wait(pe, yt_copied, c)
                    for h in range(PAIRS):
                        ins = mm(at(0, h), pbd[:, par, h], gct[:, par, h, HD:2 * HD], start=True, stop=True)
                    ins.then_inc(y_ready, 1)
                step(0)
                if b and not a:
                    inverse_applied()
                    operator()
                if e:
                    wait(pe, x3_ready, f + 1)
                    for part in range(2):
                        for t in range(KT):
                            ins = mm(bank[5][:, P * (2 * part + t):P * (2 * part + t + 1)],
                                     x3split[:, part, P * t:P * (t + 1)], ident16[:], start=True, stop=True)
                    ins.then_inc(y3t_ready, 1)
                if a:
                    wait(pe, y_copied, c + 1)
                    wait(pe, y2_copied, c)
                    for h in range(PAIRS):
                        ins = mm(at(1, h), gbd[:, par, h], ysb[:, h], start=True, stop=True)
                    ins.then_inc(g1_ready, 1)
                step(1)
                if e:
                    wait(pe, y3t_copied, f + 1)
                    hidden(0)
                if a:
                    wait(pe, r1_done, c + 1)
                    wait(pe, w_copied, c)
                    for h in range(PAIRS):
                        ins = mm(at(2, h), sbd[:, par, h], rsb[:, h], start=h == 0, stop=False, skip_group_check=True)
                    ins.then_inc(w2_ready, 1)
                step(2)
                if e:
                    hidden(1)
                if b and not a:
                    attend()
                if a:
                    wait(pe, w2_copied, c + 1)
                    for h in range(PAIRS):
                        ins = mm(at(1, h), gbd[:, par, h], w2sb[:, h], start=True, stop=True)
                    ins.then_inc(g2_ready, 1)
                step(3)
                if a and b:
                    inverse_applied()
                if a:
                    wait(pe, r2_done, c + 1)
                    for h in range(PAIRS):
                        ins = mm(at(2, h), pbd[:, par, h], r2sb[:, h], start=False, stop=h == PAIRS - 1, skip_group_check=True)
                    ins.then_inc(w_ready, 1)
                step(4)
                if e:
                    output(0)
                if a and b:
                    operator()
                if e:
                    output(1)
                if a:
                    wait(pe, wbd_copied, 2 * (c + 1))
                    wait(pe, z_copied, c)
                    wait(pe, m_copied, c)
                    for n in range(2):
                        for h in range(4):
                            ins = nc.tensor.transpose(at(3 + n, h, P), wbd[:, 4 * n + h], ident[:])
                        ins.then_inc(wbdt_ready, 1)
                step(5)
                if a and b:
                    attend()
                if a:
                    wait(pe, w_copied, c + 1)
                    for h in range(PAIRS):
                        wait(pe, wbdt_copied, 2 * c + h // 4 + 1)
                        o = 32 * (h // 2)
                        ins = mm(bank[0][o:o + 2 * RANK, P * (h % 2):P * (h % 2 + 1)], we[:, h], wbdt[:, h],
                                 start=True, stop=True)
                    ins.then_inc(yt_ready, 1)
                step(6)
                if b:
                    wait(pe, scaled, d)
                    project_out(0)
                if a:
                    wait(pe, yt_copied, c + 1)
                    for n in range(2):
                        ins = nc.tensor.transpose(at(1, n, P), yts[:, par, P * n:P * (n + 1)], ident[:])
                    ins.then_inc(y2_ready, 1)
                step(7)
                if b:
                    project_out(1)
                if a:
                    wait(pe, y2_copied, c + 1)
                    for h in range(PAIRS):
                        o = 32 * (h // 2)
                        ins = mm(bank[3][o:o + 2 * RANK, HD * (h % 2):HD * (h % 2 + 1)], factor(h), wt[:, h],
                                 start=True, stop=True)
                    ins.then_inc(z_ready, 1)
                    for h in range(PAIRS):
                        o = 2 * RANK * h
                        ins = mm(bank[4][0:2 * RANK, o:o + 2 * RANK], factor(h), factor(h), start=True, stop=True)
                    ins.then_inc(m_ready, 1)
                step(8)

            def project_all(b):
                first, last = PAIRS_B * b, PAIRS_B * (b + 1)
                for par in range(2):
                    project(first, par, True)
                with pe.Fori(first + 1, last) as i:
                    for par in range(2):
                        project(i, par, False)
                gram(last - 1, 1)

            projected = formed = 0
            applied = 0
            for stage, *at in merged(PROGRAM):
                if stage == "project":
                    project_all(*at)
                    projected += CPB
                elif stage == "schur":
                    wait(pe, h_copied, FT * (applied - 1))
                    wait(pe, ot_copied, 2 * applied)
                    pe.wait_ge(eye_placed, 4)
                    each_two_pairs(pe, at[0], schur)
                    formed += CPB
                elif stage == "joint":
                    pe.wait_ge(gc_copied, 2 * projected)
                    pe.wait_ge(kvq_copied, 6 * projected)
                    pe.wait_ge(schur_copied, formed)
                    lo, hi = at

                    def beside(solved, attended, fed, lead=False):
                        i, par = solved
                        chunk(solved, None, None, lambda n: project_step(i + BESIDE, par, lead, n))

                    for par in range(2):
                        beside((lo, par), None, None, par == 0)
                    fused_pairs(pe, lo + 1, hi, beside)
                    last = 2 * (hi + BESIDE)
                    pe.wait_ge(kvq_copied, 6 * last)
                    for j in range(2):
                        pe.wait_ge(gc_copied, 2 * last - 2 + j)
                        half_gram(1, j, bank[5])
                    projected += CPB
                elif stage == "fused":
                    pe.wait_ge(gc_copied, 2 * projected)
                    pe.wait_ge(kvq_copied, 6 * projected)
                    pe.wait_ge(schur_copied, formed)
                    pe.wait_ge(ident16_done, 1)
                    fused_pairs(pe, *at, chunk)
                    applied = 2 * max(at[1] - LAG, 0)
            chunk(None, None, LAST)


_INS = ["L0_attn_x", "L0_attn_ln_g", "L0_attn_ln_b", "L0_attn_Wq", "L0_attn_Wk", "L0_attn_Wv", "L0_attn_Wo",
        "L0_ffn_w1", "L0_ffn_b1", "L0_ffn_w2", "L0_ffn_b2"]


def kernel(**inputs):
    import numpy as _np
    import concourse.bacc as _bacc
    from concourse import mybir as _mybir
    from concourse.bass_utils import run_bass_kernel_spmd as _run

    nc = _bacc.Bacc("TRN2", target_bir_lowering=False, num_devices=1)
    arrays, args = {}, []
    for name in _INS:
        a = _np.ascontiguousarray(inputs[name])
        arrays[f"in_{name}_dram"] = a
        args.append(nc.dram_tensor(f"in_{name}_dram", a.shape, _mybir.dt.from_np(a.dtype), kind="ExternalInput").ap())
    args.append(nc.dram_tensor("out_0_dram", (BATCH, SEQ, DM), _mybir.dt.float32, kind="ExternalOutput").ap())
    build(nc, *args)
    r = _run(nc, [arrays], core_ids=[0])
    return r.results[0]["out_0_dram"]
```
